# Optimizing a Trainium2 kernel written in Bass

```python
import numpy as np
import jax
import jax.numpy as jnp

def _softmax(x, axis=-1):
    return jax.nn.softmax(x, axis=axis)

def _gelu(x):
    return jax.nn.gelu(x, approximate=True)

def _silu(x):
    return jax.nn.silu(x)

def _sigmoid(x):
    return jax.nn.sigmoid(x)

def _layernorm(x, axis=-1, eps=1e-05):
    m = jnp.mean(x, axis=axis, keepdims=True)
    v = jnp.var(x, axis=axis, keepdims=True)
    return (x - m) / jnp.sqrt(v + eps)

def _scatter_add(tgt, idx, src, axis=0):
    return tgt.at[idx].add(src)

def _segment_sum(src, seg, n):
    return jax.ops.segment_sum(src, seg, n)
kernel_name = 'mk_adj_preln_d4_adj_r2_51d76a'

def setup_inputs(seed: int=0):
    np.random.seed(seed)
    _w = jnp.asarray

    def _rec_inputs():
        import jax
        import jax.numpy as jnp
        _gk = jax.random.key(seed)
        x = -1.394e-06 + 0.9999 * jax.random.normal(jax.random.fold_in(_gk, 1), (64, 128, 256), jnp.float32)
        _a = jax.random.bernoulli(jax.random.fold_in(_gk, 2), 0.125, (64, 128, 128))
        adj = _a.astype(jnp.int32)
        return (x, adj)
    x, adj = _rec_inputs()

    def _L0_gnn_setup():
        import jax, jax.numpy as jnp
        import numpy as np
        NEG_INF = -1000000000.0
        NEG_SLOPE = 0.2

        def gat_layer(x, mask, W, a_src, a_dst, bias, concat):
            B, N, _ = x.shape
            H, F = a_src.shape
            xl = (x @ W).reshape(B, N, H, F)
            asrc = jnp.einsum('bnhf,hf->bnh', xl, a_src)
            adst = jnp.einsum('bnhf,hf->bnh', xl, a_dst)
            e = jax.nn.leaky_relu(asrc[:, :, None, :] + adst[:, None, :, :], NEG_SLOPE)
            e = jnp.where(mask[..., None], e, NEG_INF)
            attn = jax.nn.softmax(e, axis=1)
            out = jnp.einsum('bsdh,bshf->bdhf', attn, xl)
            if concat:
                out = out.reshape(B, N, H * F)
            else:
                out = out.mean(axis=2)
            return out + bias
        key = jax.random.key(seed)
        ks = jax.random.split(key, 10)
        B, N, Din, Fh, H, Dout = (8, 512, 256, 128, 4, 256)
        s = 0.05
        return {'adj': jax.random.randint(ks[0], (B, N, N), 0, 2, dtype=jnp.int32), 'x': jax.random.normal(ks[1], (B, N, Din), dtype=jnp.float32), 'W1': jax.random.normal(ks[2], (Din, H * Fh), dtype=jnp.float32) * s, 'att_src1': jax.random.normal(ks[3], (H, Fh), dtype=jnp.float32) * s, 'att_dst1': jax.random.normal(ks[4], (H, Fh), dtype=jnp.float32) * s, 'b1': jax.random.normal(ks[5], (H * Fh,), dtype=jnp.float32) * s, 'W2': jax.random.normal(ks[6], (H * Fh, Dout), dtype=jnp.float32) * s, 'att_src2': jax.random.normal(ks[7], (1, Dout), dtype=jnp.float32) * s, 'att_dst2': jax.random.normal(ks[8], (1, Dout), dtype=jnp.float32) * s, 'b2': jax.random.normal(ks[9], (Dout,), dtype=jnp.float32) * s}
    _L0_gnn_all = _L0_gnn_setup()
    _L0_gnn_in = {k: v for k, v in _L0_gnn_all.items() if k in ('W1', 'att_src1', 'att_dst1', 'b1', 'W2', 'att_src2', 'att_dst2', 'b2')}
    del _L0_gnn_all

    def _L1_gnn_setup():
        import jax, jax.numpy as jnp
        import numpy as np
        B, N, DIN, DOUT = (8, 1024, 256, 256)
        key = jax.random.key(seed)
        kx, ka, kw, kb, kattn = jax.random.split(key, 5)
        x = jax.random.normal(kx, (B, N, DIN), dtype=jnp.float32)
        adjacency_matrix = jax.random.randint(ka, (B, N, N), 0, 2, dtype=jnp.int32)
        lim_w = float(np.sqrt(1.0 / DIN))
        W = jax.random.uniform(kw, (DOUT, DIN), minval=-lim_w, maxval=lim_w, dtype=jnp.float32)
        b = jax.random.uniform(kb, (DOUT,), minval=-lim_w, maxval=lim_w, dtype=jnp.float32)
        lim_a = float(np.sqrt(6.0 / (DOUT + DOUT)))
        attn = jax.random.uniform(kattn, (DOUT, DOUT), minval=-lim_a, maxval=lim_a, dtype=jnp.float32)
        return {'x': x, 'adjacency_matrix': adjacency_matrix, 'W': W, 'b': b, 'attn': attn}
    _L1_gnn_all = _L1_gnn_setup()
    _L1_gnn_in = {k: v for k, v in _L1_gnn_all.items() if k in ('W', 'b', 'attn')}
    del _L1_gnn_all

    def _L2_gnn_setup():
        import jax, jax.numpy as jnp
        import numpy as np
        ALPHA = 0.2
        K_NUM = 16
        NEG_INF = -9000000000000000.0
        key = jax.random.key(seed)
        k1, k2, k3, k4 = jax.random.split(key, 4)
        B, N, F_in, F_out = (4, 1024, 256, 256)
        h = jax.random.normal(k1, (B, N, F_in), dtype=jnp.float32)
        adj = jax.random.randint(k2, (B, N, N), 0, 2, dtype=jnp.int32)

        def xavier(k, shape, gain=1.414):
            fan_in, fan_out = (shape[0], shape[1])
            bound = gain * np.sqrt(6.0 / (fan_in + fan_out))
            return jax.random.uniform(k, shape, jnp.float32, -bound, bound)
        W = xavier(k3, (F_in, F_out))
        a = xavier(k4, (2 * F_out, 1))
        return {'h': h, 'adj': adj, 'W': W, 'a': a}
    _L2_gnn_all = _L2_gnn_setup()
    _L2_gnn_in = {k: v for k, v in _L2_gnn_all.items() if k in ('W', 'a')}
    del _L2_gnn_all

    def _L3_gnn_setup():
        import jax, jax.numpy as jnp
        import numpy as np
        NEG_INF = -1000000000.0
        ALPHA = 0.1
        key = jax.random.key(seed)
        k1, k2, k3, k4, k5 = jax.random.split(key, 5)
        B, N, Din, Dout = (8, 1024, 256, 256)
        features = jax.random.normal(k1, (B, N, Din), dtype=jnp.float32)
        graph = jax.random.randint(k2, (B, N, N), 0, 2, dtype=jnp.int64)
        lim_w = 1.414 * np.sqrt(6.0 / (Din + Dout))
        w = jax.random.uniform(k3, (Din, Dout), jnp.float32, -lim_w, lim_w)
        lim_a = 1.414 * np.sqrt(6.0 / (Dout + 1))
        a1 = jax.random.uniform(k4, (Dout, 1), jnp.float32, -lim_a, lim_a)
        a2 = jax.random.uniform(k5, (Dout, 1), jnp.float32, -lim_a, lim_a)
        return {'features': features, 'graph': graph, 'w': w, 'a1': a1, 'a2': a2}
    _L3_gnn_all = _L3_gnn_setup()
    _L3_gnn_in = {k: v for k, v in _L3_gnn_all.items() if k in ('w', 'a1', 'a2')}
    del _L3_gnn_all
    return {'x': x, 'adj': adj, 'L0_gnn_W1': _L0_gnn_in['W1'], 'L0_gnn_att_src1': _L0_gnn_in['att_src1'], 'L0_gnn_att_dst1': _L0_gnn_in['att_dst1'], 'L0_gnn_b1': _L0_gnn_in['b1'], 'L0_gnn_W2': _L0_gnn_in['W2'], 'L0_gnn_att_src2': _L0_gnn_in['att_src2'], 'L0_gnn_att_dst2': _L0_gnn_in['att_dst2'], 'L0_gnn_b2': _L0_gnn_in['b2'], 'L1_gnn_W': _L1_gnn_in['W'], 'L1_gnn_b': _L1_gnn_in['b'], 'L1_gnn_attn': _L1_gnn_in['attn'], 'L2_gnn_W': _L2_gnn_in['W'], 'L2_gnn_a': _L2_gnn_in['a'], 'L3_gnn_w': _L3_gnn_in['w'], 'L3_gnn_a1': _L3_gnn_in['a1'], 'L3_gnn_a2': _L3_gnn_in['a2']}

def reference(x, adj, L0_gnn_W1, L0_gnn_att_src1, L0_gnn_att_dst1, L0_gnn_b1, L0_gnn_W2, L0_gnn_att_src2, L0_gnn_att_dst2, L0_gnn_b2, L1_gnn_W, L1_gnn_b, L1_gnn_attn, L2_gnn_W, L2_gnn_a, L3_gnn_w, L3_gnn_a1, L3_gnn_a2):
    import jax
    import jax.numpy as jnp

    def _L0_gnn_ref(adj, x, W1, att_src1, att_dst1, b1, W2, att_src2, att_dst2, b2):
        import jax, jax.numpy as jnp
        import numpy as np
        NEG_INF = -1000000000.0
        NEG_SLOPE = 0.2

        def gat_layer(x, mask, W, a_src, a_dst, bias, concat):
            B, N, _ = x.shape
            H, F = a_src.shape
            xl = (x @ W).reshape(B, N, H, F)
            asrc = jnp.einsum('bnhf,hf->bnh', xl, a_src)
            adst = jnp.einsum('bnhf,hf->bnh', xl, a_dst)
            e = jax.nn.leaky_relu(asrc[:, :, None, :] + adst[:, None, :, :], NEG_SLOPE)
            e = jnp.where(mask[..., None], e, NEG_INF)
            attn = jax.nn.softmax(e, axis=1)
            out = jnp.einsum('bsdh,bshf->bdhf', attn, xl)
            if concat:
                out = out.reshape(B, N, H * F)
            else:
                out = out.mean(axis=2)
            return out + bias
        B, N, _ = adj.shape
        mask = (adj > 0) | jnp.eye(N, dtype=bool)[None]
        h = jax.nn.elu(gat_layer(x, mask, W1, att_src1, att_dst1, b1, concat=True))
        h = gat_layer(h, mask, W2, att_src2, att_dst2, b2, concat=False)
        return h

    def _L1_gnn_ref(x, adjacency_matrix, W, b, attn):
        import jax, jax.numpy as jnp
        import numpy as np
        B, N, DIN, DOUT = (8, 1024, 256, 256)
        h = jnp.einsum('bni,oi->bno', x, W) + b
        ha = jnp.einsum('bmi,ij->bmj', h, attn)
        scores = jnp.einsum('bmj,bnj->bmn', ha, h)
        scores = jnp.where(adjacency_matrix == 0, -jnp.inf, scores)
        attn_weights = jax.nn.softmax(scores, axis=-1)
        x_out = jnp.einsum('bmn,bnd->bmd', attn_weights, h)
        return jax.nn.elu(x_out)

    def _L2_gnn_ref(h, adj, W, a):
        import jax, jax.numpy as jnp
        import numpy as np
        ALPHA = 0.2
        K_NUM = 16
        NEG_INF = -9000000000000000.0
        F_out = W.shape[1]
        Wh = jnp.einsum('bnf,fo->bno', h, W)
        a1, a2 = (a[:F_out, 0], a[F_out:, 0])
        e_src = Wh @ a1
        e_dst = Wh @ a2
        e = e_src[:, :, None] + e_dst[:, None, :]
        e = jnp.where(e > 0, e, ALPHA * e)
        e = jnp.where(adj > 0, e, NEG_INF)
        attention = jax.nn.softmax(e, axis=2)
        topk_vals = jax.lax.top_k(attention, K_NUM)[0]
        kth = topk_vals[:, :, -1:]
        attention = jnp.where(attention < kth, 0.0, attention)
        h_prime = jnp.einsum('bij,bjo->bio', attention, Wh)
        return jax.nn.elu(h_prime)

    def _L3_gnn_ref(features, graph, w, a1, a2):
        import jax, jax.numpy as jnp
        import numpy as np
        NEG_INF = -1000000000.0
        ALPHA = 0.1
        hidden = jnp.einsum('bni,io->bno', features, w)
        s1 = hidden @ a1
        s2 = hidden @ a2
        e = jax.nn.leaky_relu(s1 + jnp.swapaxes(s2, 1, 2), negative_slope=ALPHA)
        e = jnp.where(graph == 0, NEG_INF, e)
        attn = jax.nn.softmax(e, axis=-1)
        h_prime = jnp.einsum('bij,bjo->bio', attn, hidden)
        return jax.nn.elu(h_prime)
    h = jnp.maximum(_layernorm(x, axis=-1), 0.0)
    x = x + _L0_gnn_ref(adj, h, L0_gnn_W1, L0_gnn_att_src1, L0_gnn_att_dst1, L0_gnn_b1, L0_gnn_W2, L0_gnn_att_src2, L0_gnn_att_dst2, L0_gnn_b2)
    h = jnp.maximum(_layernorm(x, axis=-1), 0.0)
    x = x + _L1_gnn_ref(h, adj, L1_gnn_W, L1_gnn_b, L1_gnn_attn)
    h = jnp.maximum(_layernorm(x, axis=-1), 0.0)
    x = x + _L2_gnn_ref(h, adj, L2_gnn_W, L2_gnn_a)
    h = jnp.maximum(_layernorm(x, axis=-1), 0.0)
    x = x + _L3_gnn_ref(h, adj, L3_gnn_w, L3_gnn_a1, L3_gnn_a2)
    return x

_drawn_inputs = setup_inputs


def setup_inputs(seed=0):
    import zlib

    import numpy as np

    out = dict(_drawn_inputs(seed))
    spreads = {}
    factors = {'L0_gnn_att_src1': 4.516,
     'L0_gnn_att_dst1': 29.081,
     'L0_gnn_att_src2': 8.0,
     'L0_gnn_att_dst2': 62.456,
     'L3_gnn_a1': 3.073}
    for name, (base, spread) in spreads.items():
        noise = np.random.default_rng([zlib.crc32(name.encode()), seed]).standard_normal(out[name].shape)
        drawn = base * np.exp(spread * noise) if base else spread * noise
        out[name] = jnp.asarray(drawn.astype(out[name].dtype))
    for name, factor in factors.items():
        out[name] = (out[name] * factor).astype(out[name].dtype)
    return out
```

```python
from collections import namedtuple
from contextlib import ExitStack

import numpy as np

import concourse.bass as bass
import concourse.mybir as mybir

F32 = mybir.dt.float32
BF16 = mybir.dt.bfloat16
I32 = mybir.dt.int32
ALU = mybir.AluOpType
ACT = mybir.ActivationFunctionType
AX = mybir.AxisListType

GRAPHS, NODES, DIM = 64, 128, 256
P = 128
G = 2
PAIRS = GRAPHS // G
KC = DIM // P
HEADS, HF = 4, 128
HID = HEADS * HF
NEG = -1e30
EPS = 1e-5
SLOPE_L0, SLOPE_L2, SLOPE_L3 = 0.2, 0.2, 0.1
TOPK_ROUNDS = 2
BANKS = 8
HI, MID, LO = 0, 64, 96

LOOP_FROM = 6
LAST_LAG = 5
STORE_LAG = 5
WEIGHT_LOADS = 18

Pair = namedtuple("Pair", "n par")


def lagged(turn, lag):
    return Pair(turn.n - lag, (turn.par - lag) % 2)


def live(p):
    return not isinstance(p.n, int) or 0 <= p.n < PAIRS


def graph_layers(nc, x, adj, w1, src1, dst1, b1, w2, src2, dst2, b2, wl, bl, al, w3, a3, w4, a4src, a4dst, out):
    with ExitStack() as ctx:
        def sb(name, shape, dt=F32):
            return ctx.enter_context(nc.sbuf_tensor(name, shape, dt))

        def two(name, shape, dt=F32):
            return sb(name, [P, 2, *shape], dt)

        sems = {}

        def sem(name):
            if name not in sems:
                sems[name] = ctx.enter_context(nc.semaphore(name))
            return sems[name]

        def wait(eng, name, p, back=0):
            n = p.n + 1 - back
            if isinstance(n, int):
                n = min(n, PAIRS)
                if n < 1:
                    return
            eng.wait_ge(sem(name), n)

        def have(eng, *values):
            for v in values:
                if not isinstance(v, int):
                    eng.compute_val(v)

        ident = sb("ident", [P, P])
        ident_bf = sb("ident_bf", [P, P], BF16)
        ones = sb("ones", [P, P])
        offdiag = sb("offdiag", [P, P])
        pick_src = sb("pick_src", [P, HEADS, P], BF16)
        pick_dst = sb("pick_dst", [P, HEADS, P], BF16)
        minus1 = sb("minus1", [P, 1])
        minus_half = sb("minus_half", [P, G])
        w1_s = sb("w1_s", [P, KC, HID])
        coef_w = sb("coef_w", [P, KC, P])
        b1_s = sb("b1_s", [P, HID])
        w2_s = sb("w2_s", [P, HEADS, DIM + 2])
        b2_s = sb("b2_s", [P, DIM + 2])
        wl_s = sb("wl_s", [P, KC, DIM])
        al_s = sb("al_s", [P, KC, DIM])
        bl_col = sb("bl_col", [P, KC])
        t1_s = sb("t1_s", [P, KC, DIM])
        ab_s = sb("ab_s", [P, KC])
        m_s = sb("m_s", [P, KC, DIM])
        c_s = sb("c_s", [P, KC])
        wv_s = sb("wv_s", [P, KC, DIM + 1])
        bv_s = sb("bv_s", [P, DIM + 1])
        w3_s = sb("w3_s", [P, KC, DIM + 2])
        w4_s = sb("w4_s", [P, KC, DIM + 2])
        mask0 = two("mask0", [G, NODES], BF16)
        masks = sb("masks", [P, GRAPHS, NODES], BF16)
        early = masks[:, :, :].rearrange("p g n -> p (g n)").bitcast(F32)
        rows1 = early[:, 0:2 * HID].rearrange("p (j n) -> p j n", j=2)
        rows = early[:, 2 * HID:2 * HID + 6 * DIM].rearrange("p (j n) -> p j n", j=6)
        prod = early[:, 2 * HID + 6 * DIM:2 * HID + 6 * DIM + HEADS * DIM].rearrange("p (h n) -> p h n", h=HEADS)
        adj_s = two("adj_s", [G, NODES], I32)
        res = [two(f"res{k}", [G, DIM]) for k in range(5)]
        stats = [two(f"stats{k}", [G, 6]) for k in range(4)]
        mv = [two(f"mv{k}", [G, 2]) for k in range(4)]
        nmean = [two(f"nmean{k}", [G]) for k in range(4)]
        vare = [two(f"vare{k}", [G]) for k in range(4)]
        rstd = [two(f"rstd{k}", [G]) for k in range(4)]
        norm = [two(f"norm{k}", [G, DIM]) for k in range(4)]
        hT = [two(f"hT{k}", [KC, G * NODES]) for k in range(4)]
        parts = two("parts", [G * NODES], BF16)
        rest = two("rest", [G * NODES])
        val0 = [two(f"val0_{g}", [HID]) for g in range(G)]
        attn0 = [two(f"attn0_{g}", [HEADS, NODES]) for g in range(G)]
        nmax0 = [two(f"nmax0_{g}", [HEADS]) for g in range(G)]
        den0 = [two(f"den0_{g}", [HEADS]) for g in range(G)]
        rden0 = [two(f"rden0_{g}", [HEADS]) for g in range(G)]
        attnT0 = [two(f"attnT0_{g}", [HEADS, NODES]) for g in range(G)]
        hid = [two(f"hid_{g}", [HID]) for g in range(G)]
        val = {X: two(f"val{X}", [G, DIM + 2]) for X in "BCDE"}
        nmax = {X: two(f"nmax{X}", [G]) for X in "BCDE"}
        mxu = two("mxu", [G])
        mx = {X: two(f"mx{X}", [G]) for X in "BCDE"}
        den = {X: two(f"den{X}", [G]) for X in "BCDE"}
        rden = {X: two(f"rden{X}", [G]) for X in "BCDE"}
        prob = {X: two(f"prob{X}", [G * NODES]) for X in "BCDE"}
        probT = {X: two(f"probT{X}", [G * NODES]) for X in "BCDE"}
        qT = two("qT", [KC, G * NODES])
        top = [two(f"top_{g}", [TOPK_ROUNDS, 8]) for g in range(G)]
        left = [two(f"left_{g}", [NODES]) for g in range(G)]
        kept = two("kept", [G * NODES])
        pos = {X: two(f"pos{X}", [G * DIM]) for X in "CDE"}
        elu = {X: two(f"elu{X}", [G * DIM]) for X in "CDE"}

        ps = ctx.enter_context(nc.psum_tensor("ps", [P, BANKS, 512], F32))

        bank_of = {"wE0": 0, "pt1": 1, "gt": 2, "zE": 3, "pt0": 4, "v1": 5, "ptD": 6, "v0": 0, "oD": 1, "sC": 2, "ot0": 3, "ot1": 4, "ptC": 5, "tr0": 6, "ptE": 0, "oC": 1, "xm0": 2, "xm1": 3, "as": 4, "zB": 5, "tr3": 6, "xl1": 0, "oE": 1, "z1": 2, "ptB": 3, "z0": 4, "tr2": 5, "oB": 6, "wD1": 0, "wD0": 1, "wE1": 2, "zD": 3, "xl0": 4, "tr1": 5}

        x_v = x.rearrange("(q g) n f -> q n g f", g=G)
        adj_v = adj.rearrange("(q g) m n -> q m g n", g=G)
        out_v = out.rearrange("(q g) n f -> q n g f", g=G)
        SLOPE = {"B": SLOPE_L0, "D": SLOPE_L2, "E": SLOPE_L3}
        LAYER = {"C": 1, "D": 2, "E": 3}

        def graph_cols(tile, par, g, n=NODES):
            return tile[:, par, g * n:(g + 1) * n]

        W2_SUM, T1_SUM, AB_SUM, WL_TURNED, M_SUM, C_SUM = range(1, 7)

        block = ctx.enter_context(nc.Block())

        def over_turns(eng, turn):
            for t in range(LOOP_FROM):
                turn(Pair(t, t % 2))
            with eng.Fori(LOOP_FROM // 2, PAIRS // 2) as i:
                turn(Pair(i * 2, 0))
                turn(Pair(i * 2 + 1, 1))
            for t in range(PAIRS, PAIRS + LAST_LAG):
                turn(Pair(t, t % 2))

        @block.sync
        def _(sp):
            def load(dst, src, **how):
                sp.dma_start(dst, src, **how).then_inc(sem("weights_in"), 16)

            def bcast(v, n):
                return v.rearrange("(a n) -> a n", a=1).to_broadcast([P, n])

            load(w1_s[:, :, :], w1.rearrange("(c k) n -> k c n", k=P))
            load(rows1[:, 0, :], bcast(src1.rearrange("h f -> (h f)"), HID))
            load(rows1[:, 1, :], bcast(dst1.rearrange("h f -> (h f)"), HID))
            load(b1_s[:, :], bcast(b1, HID))
            load(w2_s[:, :, 0:DIM], w2.rearrange("(h f) o -> f h o", f=P))
            load(rows[:, 0, :], bcast(src2.rearrange("h f -> (h f)"), DIM))
            load(rows[:, 1, :], bcast(dst2.rearrange("h f -> (h f)"), DIM))
            load(b2_s[:, 0:DIM], bcast(b2, DIM))
            load(wl_s[:, :, :], wl.rearrange("(c k) i -> k c i", k=P))
            load(al_s[:, :, :], al.rearrange("(c k) j -> k c j", k=P))
            load(bl_col[:, :], bl.rearrange("(c k) -> k c", k=P), allow_slow_non_contiguous=True)
            load(bv_s[:, 0:DIM], bcast(bl, DIM))
            load(w3_s[:, :, 0:DIM], w3.rearrange("(c k) o -> k c o", k=P))
            load(rows[:, 2, :], bcast(a3[0:DIM].rearrange("n a -> (n a)"), DIM))
            load(rows[:, 3, :], bcast(a3[DIM:2 * DIM].rearrange("n a -> (n a)"), DIM))
            load(w4_s[:, :, 0:DIM], w4.rearrange("(c k) o -> k c o", k=P))
            load(rows[:, 4, :], bcast(a4src.rearrange("n a -> (n a)"), DIM))
            load(rows[:, 5, :], bcast(a4dst.rearrange("n a -> (n a)"), DIM))

            def load_pair(p):
                if not live(p):
                    return
                wait(sp, "rsB", p, back=2)
                sp.dma_start(res[0][:, p.par, :, :], x_v[p.n] if isinstance(p.n, int) else x_v[bass.ds(p.n, 1)].rearrange("a n g f -> (a n) g f"))\
                    .then_inc(sem(f"x_in{p.par}"), 16)
                wait(sp, "mk", p, back=2)
                sp.dma_start(adj_s[:, p.par, :, :], adj_v[p.n] if isinstance(p.n, int) else adj_v[bass.ds(p.n, 1)].rearrange("a n g f -> (a n) g f"))\
                    .then_inc(sem(f"adj_in{p.par}"), 16)

            def store_pair(p):
                if not live(p):
                    return
                wait(sp, "finE", p)
                sp.dma_start(out_v[p.n] if isinstance(p.n, int) else out_v[bass.ds(p.n, 1)].rearrange("a n g f -> (a n) g f"), res[4][:, p.par, :, :])\
                    .then_inc(sem(f"stored{p.par}"), 16)

            def turn(t):
                done = lagged(t, STORE_LAG)
                have(sp, t.n - 1, done.n + 1)
                load_pair(t)
                store_pair(done)

            over_turns(sp, turn)
            for par in range(2):
                sp.wait_ge(sem(f"stored{par}"), 16 * (PAIRS // 2))

        def dma_count(p):
            n = p.n - p.par
            return 16 * (n // 2 + 1) if isinstance(n, int) else n * 8 + 16

        @block.gpsimd
        def _(pool):
            made = sem("pool_made")
            steps = [0]

            def chain(ins):
                steps[0] += 1
                ins.then_inc(made, 1)
                pool.wait_ge(made, steps[0])

            def diagonal(tile, fill, pattern, offset):
                chain(nc.gpsimd.affine_select(out=tile, in_=tile, compare_op=ALU.not_equal, fill=fill, base=-offset,
                                              pattern=pattern, channel_multiplier=1))

            for tile, value in ((ident, 0.0), (ident_bf, 0.0), (ones, 1.0), (offdiag, NEG), (pick_src, 0.0),
                                (pick_dst, 0.0), (minus1, -1.0), (minus_half, -0.5)):
                whole = tile[:, :] if len(tile.shape) == 2 else tile[:, :, :]
                chain(nc.gpsimd.memset(whole, value))
            diagonal(ident[:, :], 1.0, [[-1, P]], 0)
            diagonal(ident_bf[:, :], 1.0, [[-1, P]], 0)
            diagonal(offdiag[:, :], 0.0, [[-1, P]], 0)
            for start in (HI, MID, LO):
                diagonal(pick_src[:, :, :], 1.0, [[-1, HEADS], [0, P]], start)
                diagonal(pick_dst[:, :, :], 1.0, [[-1, HEADS], [0, P]], start + HEADS)
            nc.gpsimd.memset(coef_w[:, :, :], 0.0).then_inc(sem("constants"), 1)

            def reciprocal_std(k, p):
                if not live(p):
                    return
                wait(pool, f"aggr{k}", p)
                nc.gpsimd.tensor_tensor(rstd[k][:, p.par, :], vare[k][:, p.par, :], minus_half[:, :], ALU.pow)\
                    .then_inc(sem(f"pow{k}"), 1)

            def normalise(k, p):
                if not live(p):
                    return
                have(pool, p.n + 1)
                pool.wait_ge(sem("constants"), 1)
                wait(pool, f"pow{k}", p)
                for g in range(G):
                    ins = nc.gpsimd.tensor_scalar(norm[k][:, p.par, g, :], res[k][:, p.par, g, :],
                                                  nmean[k][:, p.par, g:g + 1], rstd[k][:, p.par, g:g + 1],
                                                  ALU.add, ALU.mult)
                ins.then_inc(sem(f"norm{k}"), 1)

            def attention_weights(g, p):
                if not live(p):
                    return
                wait(pool, f"rd{g}", p)
                nc.gpsimd.tensor_tensor(attn0[g][:, p.par, :, :], attn0[g][:, p.par, :, :],
                                        rden0[g][:, p.par, :].unsqueeze(2).to_broadcast([P, HEADS, NODES]),
                                        ALU.mult).then_inc(sem(f"nr{g}"), 1)

            def add_residual(X, p):
                if not live(p):
                    return
                k = LAYER[X]
                wait(pool, f"t{X}", p)
                if X != "E":
                    wait(pool, {"C": "finD", "D": "finE"}[X], p, back=2)
                if X == "E" and not (isinstance(p.n, int) and p.n < 2):
                    pool.wait_ge(sem(f"stored{p.par}"), dma_count(p) - 16)
                nc.gpsimd.tensor_tensor(res[k + 1][:, p.par, :, :].rearrange("p g f -> p (g f)"),
                                        res[k][:, p.par, :, :].rearrange("p g f -> p (g f)"),
                                        elu[X][:, p.par, :], ALU.add).then_inc(sem(f"fin{X}"), 1)

            def turn(t):
                reciprocal_std(0, lagged(t, 0))
                normalise(0, lagged(t, 0))
                add_residual("D", lagged(t, 3))
                reciprocal_std(3, lagged(t, 3))
                add_residual("C", lagged(t, 2))
                normalise(3, lagged(t, 3))
                reciprocal_std(2, lagged(t, 2))
                normalise(2, lagged(t, 2))
                reciprocal_std(1, lagged(t, 1))
                normalise(1, lagged(t, 1))
                attention_weights(1, lagged(t, 0))
                attention_weights(0, lagged(t, 0))
                add_residual("E", lagged(t, 4))

            over_turns(pool, turn)

        @block.tensor
        def _(pe):
            def mm(out_, lhsT, rhs, start, stop):
                return nc.tensor.matmul(out_, lhsT, rhs, start=start, stop=stop)

            pe.wait_ge(sem("constants"), 1)
            pe.wait_ge(sem("weights_in"), 16 * WEIGHT_LOADS)
            for h in range(HEADS):
                if h == 0:
                    pe.wait_ge(sem("w2_ready"), 1)
                ins = mm(ps[:, 0, 0:DIM + 2], ones[:, :], w2_s[:, h, :], h == 0, h == HEADS - 1)
            ins.then_inc(sem("pe_made"), 1)
            for jc in range(KC):
                for oc in range(KC):
                    ins = mm(ps[:, 1, jc * DIM:(jc + 1) * DIM], al_s[:, oc, jc * P:(jc + 1) * P], wl_s[:, oc, :],
                             oc == 0, oc == KC - 1)
            ins.then_inc(sem("pe_made"), 1)
            for jc in range(KC):
                for oc in range(KC):
                    ins = mm(ps[:, 2, jc:jc + 1], al_s[:, oc, jc * P:(jc + 1) * P], bl_col[:, oc:oc + 1],
                             oc == 0, oc == KC - 1)
            ins.then_inc(sem("pe_made"), 1)
            for ic in range(KC):
                for oc in range(KC):
                    ins = nc.tensor.transpose(ps[:, 3, (ic * KC + oc) * P:(ic * KC + oc + 1) * P],
                                              wl_s[:, oc, ic * P:(ic + 1) * P], ident[:, :])
            ins.then_inc(sem("pe_made"), 1)
            pe.wait_ge(sem("t1_ready"), 2)
            for ic in range(KC):
                for jc in range(KC):
                    ins = mm(ps[:, 4, ic * DIM:(ic + 1) * DIM], t1_s[:, jc, ic * P:(ic + 1) * P], wl_s[:, jc, :],
                             jc == 0, jc == KC - 1)
            ins.then_inc(sem("pe_made"), 1)
            for ic in range(KC):
                for jc in range(KC):
                    mm(ps[:, 5, ic:ic + 1], wl_s[:, jc, ic * P:(ic + 1) * P], ab_s[:, jc:jc + 1], jc == 0, jc == KC - 1)
            for ic in range(KC):
                for jc in range(KC):
                    mm(ps[:, 5, KC + ic:KC + ic + 1], t1_s[:, jc, ic * P:(ic + 1) * P], bl_col[:, jc:jc + 1],
                       jc == 0, jc == KC - 1)
            for jc in range(KC):
                ins = mm(ps[:, 5, 2 * KC:2 * KC + 1], ab_s[:, jc:jc + 1].to_broadcast([P, P]), bl_col[:, jc:jc + 1],
                         jc == 0, jc == KC - 1)
            ins.then_inc(sem("pe_made"), 1)
            pe.wait_ge(sem("weights_ready"), 1)

            def bank_free(p, bank, after):
                name, turn, lag = after
                wait(pe, name, lagged(turn, lag))

            def turn_norm(k, p, bank, after):
                if not live(p):
                    return
                bank_free(p, bank, after)
                wait(pe, f"norm{k}", p)
                for c in range(KC):
                    for g in range(G):
                        ins = nc.tensor.transpose(ps[:, bank, (c * G + g) * P:(c * G + g + 1) * P],
                                                  norm[k][:, p.par, g, c * P:(c + 1) * P], ident[:, :])
                ins.then_inc(sem(f"tr{k}"), 1)

            def coefficients(p, bank, after):
                if not live(p):
                    return
                bank_free(p, bank, after)
                wait(pe, "rl0", p)
                for c in range(KC):
                    ins = mm(ps[:, bank, 0:G * NODES], coef_w[:, c, :], hT[0][:, p.par, c, :], c == 0, c == KC - 1)
                ins.then_inc(sem("as"), 1)

            def values0(g, p, bank, after):
                if not live(p):
                    return
                bank_free(p, bank, after)
                wait(pe, "rl0", p)
                for c in range(KC):
                    ins = mm(ps[:, bank, :], hT[0][:, p.par, c, g * P:(g + 1) * P], w1_s[:, c, :], c == 0, c == KC - 1)
                ins.then_inc(sem(f"xl{g}"), 1)

            def scores0(g, p, bank, after):
                if not live(p):
                    return
                bank_free(p, bank, after)
                wait(pe, "mk", p)
                wait(pe, "sp2", p)
                mm(ps[:, bank, :], mask0[:, p.par, g, :], ident_bf[:, :].unsqueeze(1).to_broadcast([P, HEADS, P]), True, False)
                mine = graph_cols(parts, p.par, g)
                mm(ps[:, bank, :], mine, pick_dst[:, :, :], False, False)
                for h in range(HEADS):
                    ins = mm(ps[:, bank, h * P:(h + 1) * P], pick_src[:, h, :], mine, False, h == HEADS - 1)
                ins.then_inc(sem(f"z{g}"), 1)

            def turn_weights0(g, p, bank, after):
                if not live(p):
                    return
                bank_free(p, bank, after)
                wait(pe, f"nr{g}", p)
                for h in range(HEADS):
                    ins = nc.tensor.transpose(ps[:, bank, h * P:(h + 1) * P], attn0[g][:, p.par, h, :], ident[:, :])
                ins.then_inc(sem(f"pt{g}"), 1)

            def attend0(g, p, bank, after):
                if not live(p):
                    return
                bank_free(p, bank, after)
                wait(pe, f"xb{g}", p)
                wait(pe, f"pc{g}", p)
                for h in range(HEADS):
                    ins = mm(ps[:, bank, h * P:(h + 1) * P], val0[g][:, p.par, h * HF:(h + 1) * HF],
                             attnT0[g][:, p.par, h, :], True, True)
                ins.then_inc(sem(f"ot{g}"), 1)

            def values_b(g, p, bank, after):
                if not live(p):
                    return
                bank_free(p, bank, after)
                wait(pe, f"eu{g}", p)
                for h in range(HEADS):
                    ins = mm(ps[:, bank, 0:DIM + 2], hid[g][:, p.par, h * P:(h + 1) * P], w2_s[:, h, :],
                             h == 0, h == HEADS - 1)
                ins.then_inc(sem(f"xm{g}"), 1)

            def values(X, g, p, bank, after):
                if not live(p):
                    return
                w = w3_s if X == "D" else w4_s
                k = LAYER[X]
                bank_free(p, bank, after)
                wait(pe, f"rl{k}", p)
                for c in range(KC):
                    ins = mm(ps[:, bank, 0:DIM + 2], hT[k][:, p.par, c, g * P:(g + 1) * P], w[:, c, :], c == 0, c == KC - 1)
                ins.then_inc(sem(f"w{X}{g}"), 1)

            def scores(X, p, bank, after):
                if not live(p):
                    return
                bank_free(p, bank, after)
                copied = ("xn0", "xn1") if X == "B" else (f"wc{X}0", f"wc{X}1")
                for name in copied:
                    wait(pe, name, p)
                row, col = (DIM + 1, DIM) if X == "B" else (DIM, DIM + 1)
                for g in range(G):
                    dst = ps[:, bank, g * P:(g + 1) * P]
                    if X == "B":
                        mm(dst, mask0[:, p.par, g, :], ident_bf[:, :], True, False)
                    else:
                        mm(dst, ident_bf[:, :], graph_mask(p, g), True, False)
                    v = val[X][:, p.par, g, :]
                    mm(dst, v[:, col:col + 1].to_broadcast([P, P]), ident[:, :], False, False)
                    ins = mm(dst, ident[:, :], v[:, row:row + 1].to_broadcast([P, P]), False, True)
                ins.then_inc(sem(f"z{X}"), 1)

            def graph_mask(p, g):
                if isinstance(p.n, int):
                    return masks[:, G * p.n + g, :]
                return masks[:, bass.ds(p.n * G + g, 1), :].rearrange("p a n -> p (a n)")

            def turn_weights(X, p, bank, after):
                if not live(p):
                    return
                bank_free(p, bank, after)
                src, name = (kept, "tk1") if X == "D" else (prob[X], f"ex{X}")
                if X == "D":
                    wait(pe, "tk0", p)
                wait(pe, name, p)
                for g in range(G):
                    ins = nc.tensor.transpose(ps[:, bank, g * P:(g + 1) * P], graph_cols(src, p.par, g), ident[:, :])
                ins.then_inc(sem(f"pt{X}"), 1)

            def attend(X, p, bank, after):
                if not live(p):
                    return
                bank_free(p, bank, after)
                wait(pe, f"pc{X}", p)
                for g in range(G):
                    ins = mm(ps[:, bank, g * DIM:(g + 1) * DIM], graph_cols(probT[X], p.par, g),
                             val[X][:, p.par, g, 0:DIM], True, True)
                ins.then_inc(sem(f"o{X}"), 1)

            def queries(p, bank, after):
                if not live(p):
                    return
                bank_free(p, bank, after)
                wait(pe, "rl1", p)
                for ic in range(KC):
                    for c in range(KC):
                        ins = mm(ps[:, bank, ic * G * P:(ic + 1) * G * P], m_s[:, c, ic * P:(ic + 1) * P],
                                 hT[1][:, p.par, c, :], c == 0, c == KC - 1)
                ins.then_inc(sem("gt"), 1)

            def values_c(g, p, bank, after):
                if not live(p):
                    return
                bank_free(p, bank, after)
                wait(pe, "rl1", p)
                for c in range(KC):
                    ins = mm(ps[:, bank, 0:DIM + 1], hT[1][:, p.par, c, g * P:(g + 1) * P], wv_s[:, c, :],
                             c == 0, c == KC - 1)
                ins.then_inc(sem(f"v{g}"), 1)

            def scores_c(p, bank, after):
                if not live(p):
                    return
                bank_free(p, bank, after)
                wait(pe, "gc", p)
                for g in range(G):
                    dst = ps[:, bank, g * P:(g + 1) * P]
                    mm(dst, ident_bf[:, :], graph_mask(p, g), True, False)
                    for c in range(KC):
                        ins = mm(dst, qT[:, p.par, c, g * P:(g + 1) * P], hT[1][:, p.par, c, g * P:(g + 1) * P],
                                 False, c == KC - 1)
                ins.then_inc(sem("sC"), 1)

            def turn(t):
                values("E", 0, lagged(t, 4), bank=bank_of["wE0"], after=("wcD1", t, 3))
                turn_weights0(1, lagged(t, 1), bank=bank_of["pt1"], after=("wcD0", t, 3))
                queries(lagged(t, 2), bank=bank_of["gt"], after=("wcE1", t, 4))
                scores("E", lagged(t, 4), bank=bank_of["zE"], after=("lkD", t, 3))
                turn_weights0(0, lagged(t, 1), bank=bank_of["pt0"], after=("xb0", t, 1))
                values_c(1, lagged(t, 2), bank=bank_of["v1"], after=("rl1", t, 2))
                turn_weights("D", lagged(t, 3), bank=bank_of["ptD"], after=("rsB", t, 2))
                values_c(0, lagged(t, 2), bank=bank_of["v0"], after=("wcE0", t, 4))
                attend("D", lagged(t, 3), bank=bank_of["oD"], after=("pc1", t, 1))
                scores_c(lagged(t, 2), bank=bank_of["sC"], after=("gc", t, 2))
                attend0(0, lagged(t, 1), bank=bank_of["ot0"], after=("lkE", t, 4))
                attend0(1, lagged(t, 1), bank=bank_of["ot1"], after=("pc0", t, 1))
                turn_weights("C", lagged(t, 2), bank=bank_of["ptC"], after=("vb1", t, 2))
                turn_norm(0, lagged(t, 0), bank=bank_of["tr0"], after=("pcD", t, 3))
                turn_weights("E", lagged(t, 4), bank=bank_of["ptE"], after=("vb0", t, 2))
                attend("C", lagged(t, 2), bank=bank_of["oC"], after=("rD", t, 3))
                values_b(0, lagged(t, 1), bank=bank_of["xm0"], after=("exC", t, 2))
                values_b(1, lagged(t, 1), bank=bank_of["xm1"], after=("eu0", t, 1))
                coefficients(lagged(t, 0), bank=bank_of["as"], after=("eu1", t, 1))
                scores("B", lagged(t, 1), bank=bank_of["zB"], after=("pcC", t, 2))
                turn_norm(3, lagged(t, 3), bank=bank_of["tr3"], after=("rl0", t, 0))
                values0(1, lagged(t, 0), bank=bank_of["xl1"], after=("pcE", t, 4))
                attend("E", lagged(t, 4), bank=bank_of["oE"], after=("rC", t, 2))
                scores0(1, lagged(t, 0), bank=bank_of["z1"], after=("xn0", t, 1))
                turn_weights("B", lagged(t, 1), bank=bank_of["ptB"], after=("xn1", t, 1))
                scores0(0, lagged(t, 0), bank=bank_of["z0"], after=("sp1", t, 0))
                turn_norm(2, lagged(t, 2), bank=bank_of["tr2"], after=("lkB", t, 1))
                attend("B", lagged(t, 1), bank=bank_of["oB"], after=("rl3", t, 3))
                values("D", 1, lagged(t, 2), bank=bank_of["wD1"], after=("xb1", t, 0))
                values("D", 0, lagged(t, 2), bank=bank_of["wD0"], after=("rE", t, 4))
                values("E", 1, lagged(t, 3), bank=bank_of["wE1"], after=("lk1", t, 0))
                scores("D", lagged(t, 2), bank=bank_of["zD"], after=("pcB", t, 1))
                values0(0, lagged(t, 0), bank=bank_of["xl0"], after=("lk0", t, 0))
                turn_norm(1, lagged(t, 1), bank=bank_of["tr1"], after=("rl2", t, 2))

            over_turns(pe, turn)

        @block.scalar
        def _(act):
            def relu_copy(k, p):
                if not live(p):
                    return
                wait(act, f"tr{k}", p)
                nc.scalar.activation(hT[k][:, p.par, :, :].rearrange("p c n -> p (c n)"), ps[:, bank_of[f"tr{k}"], :],
                                     ACT.Relu).then_inc(sem(f"rl{k}"), 1)

            def scaled0(g, p):
                if not live(p):
                    return
                wait(act, f"pt{g}", p, back=2)
                wait(act, f"z{g}", p)
                nc.scalar.activation(attn0[g][:, p.par, :, :].rearrange("p h n -> p (h n)"), ps[:, bank_of[f"z{g}"], :], ACT.Copy, scale=SLOPE_L0)\
                    .then_inc(sem(f"az{g}"), 1)

            def exponentials0(g, p):
                if not live(p):
                    return
                wait(act, f"mx{g}", p)
                for h in range(HEADS):
                    ins = nc.scalar.activation(attn0[g][:, p.par, h, :], attn0[g][:, p.par, h, :], ACT.Exp,
                                               bias=nmax0[g][:, p.par, h:h + 1], accum_out=den0[g][:, p.par, h:h + 1])
                ins.then_inc(sem(f"ex{g}"), 1)

            def copy_weights0(g, p):
                if not live(p):
                    return
                wait(act, f"pt{g}", p)
                nc.scalar.activation(attnT0[g][:, p.par, :, :].rearrange("p h n -> p (h n)"), ps[:, bank_of[f"pt{g}"], :],
                                     ACT.Copy).then_inc(sem(f"pc{g}"), 1)

            def elu_exp0(g, p):
                if not live(p):
                    return
                wait(act, f"xm{g}", p, back=2)
                wait(act, f"ot{g}", p)
                nc.scalar.activation(hid[g][:, p.par, :], ps[:, bank_of[f"ot{g}"], :], ACT.Exp, bias=minus1[:, 0:1])\
                    .then_inc(sem(f"el{g}"), 1)

            def scaled(X, p):
                if not live(p):
                    return
                wait(act, "tk1" if X == "D" else f"pt{X}", p, back=2)
                wait(act, f"z{X}", p)
                nc.scalar.activation(prob[X][:, p.par, :], ps[:, bank_of[f"z{X}"], 0:G * NODES], ACT.Copy, scale=SLOPE[X])\
                    .then_inc(sem(f"az{X}"), 1)

            def exponentials(X, p):
                if not live(p):
                    return
                wait(act, f"mx{X}", p)
                for g in range(G):
                    src = ps[:, bank_of["sC"], g * P:(g + 1) * P] if X == "C" else graph_cols(prob[X], p.par, g)
                    ins = nc.scalar.activation(graph_cols(prob[X], p.par, g), src, ACT.Exp,
                                               bias=nmax[X][:, p.par, g:g + 1], accum_out=den[X][:, p.par, g:g + 1])
                ins.then_inc(sem(f"ex{X}"), 1)

            def copy_weights(X, p):
                if not live(p):
                    return
                wait(act, f"pt{X}", p)
                nc.scalar.activation(probT[X][:, p.par, :], ps[:, bank_of[f"pt{X}"], 0:G * NODES], ACT.Copy)\
                    .then_inc(sem(f"pc{X}"), 1)

            def copy_values(X, g, p):
                if not live(p):
                    return
                wait(act, f"w{X}{g}", p)
                nc.scalar.activation(val[X][:, p.par, g, :], ps[:, bank_of[f"w{X}{g}"], 0:DIM + 2], ACT.Copy)\
                    .then_inc(sem(f"wc{X}{g}"), 1)

            def copy_queries(p):
                if not live(p):
                    return
                wait(act, "gt", p)
                for c in range(KC):
                    ins = nc.scalar.activation(qT[:, p.par, c, :], ps[:, bank_of["gt"], c * G * P:(c + 1) * G * P],
                                               ACT.Identity, bias=c_s[:, c:c + 1])
                ins.then_inc(sem("gc"), 1)

            def elu_exp(X, p):
                if not live(p):
                    return
                wait(act, f"fin{X}", p, back=2)
                wait(act, f"rd{X}", p)
                wait(act, f"o{X}", p)
                for g in range(G):
                    nc.scalar.activation(graph_cols(elu[X], p.par, g, DIM), ps[:, bank_of[f"o{X}"], g * DIM:(g + 1) * DIM],
                                               ACT.Exp, scale=rden[X][:, p.par, g:g + 1])

            def elu_relu(X, p):
                if not live(p):
                    return
                for g in range(G):
                    ins = nc.scalar.activation(graph_cols(pos[X], p.par, g, DIM), ps[:, bank_of[f"o{X}"], g * DIM:(g + 1) * DIM],
                                               ACT.Relu, scale=rden[X][:, p.par, g:g + 1])
                ins.then_inc(sem(f"r{X}"), 1)

            act.wait_ge(sem("weights_ready"), 1)

            def turn(t):
                copy_weights0(1, lagged(t, 1))
                copy_values("E", 0, lagged(t, 4))
                copy_queries(lagged(t, 2))
                scaled("E", lagged(t, 4))
                copy_weights0(0, lagged(t, 1))
                copy_weights("D", lagged(t, 3))
                exponentials("E", lagged(t, 4))
                elu_exp("D", lagged(t, 3))
                elu_relu("D", lagged(t, 3))
                exponentials("C", lagged(t, 2))
                elu_exp0(0, lagged(t, 1))
                copy_weights("C", lagged(t, 2))
                elu_exp0(1, lagged(t, 1))
                elu_exp("C", lagged(t, 2))
                elu_relu("C", lagged(t, 2))
                relu_copy(0, lagged(t, 0))
                copy_weights("E", lagged(t, 4))
                scaled("B", lagged(t, 1))
                relu_copy(3, lagged(t, 3))
                exponentials("B", lagged(t, 1))
                scaled0(1, lagged(t, 0))
                copy_weights("B", lagged(t, 1))
                elu_exp("E", lagged(t, 4))
                relu_copy(2, lagged(t, 2))
                elu_relu("E", lagged(t, 4))
                copy_values("D", 1, lagged(t, 2))
                scaled0(0, lagged(t, 0))
                copy_values("D", 0, lagged(t, 2))
                exponentials0(1, lagged(t, 0))
                copy_values("E", 1, lagged(t, 3))
                scaled("D", lagged(t, 2))
                exponentials0(0, lagged(t, 0))
                relu_copy(1, lagged(t, 1))
                exponentials("D", lagged(t, 2))

            over_turns(act, turn)

        @block.vector
        def _(dve):
            made = sem("dve_made")
            steps = [0]

            def chain(ins):
                steps[0] += 1
                ins.then_inc(made, 1)
                dve.wait_ge(made, steps[0])

            def tt(o, a, b, op):
                return nc.vector.tensor_tensor(o, a, b, op)

            dve.wait_ge(sem("constants"), 1)
            dve.wait_ge(sem("weights_in"), 16 * WEIGHT_LOADS)
            for j in range(2):
                for c in range(KC):
                    chain(tt(prod[:, 0:2, :].rearrange("p a b -> p (a b)"), w1_s[:, c, :], rows1[:, j, :], ALU.mult))
                    for start in (HI, MID, LO):
                        at = start + j * HEADS
                        chain(nc.vector.tensor_reduce(coef_w[:, c, at:at + HEADS],
                                                      prod[:, 0:2, :].rearrange("p a (h f) -> p (a h) f", f=HF), AX.X, ALU.add))
            for j in range(2):
                chain(tt(prod[:, :, :], w2_s[:, :, 0:DIM], rows[:, j:j + 1, :].to_broadcast([P, HEADS, DIM]), ALU.mult))
                chain(nc.vector.tensor_reduce(w2_s[:, :, DIM + j], prod[:, :, :], AX.X, ALU.add))
            nc.vector.tensor_scalar(b1_s[:, :], b1_s[:, :], 1.0, None, ALU.add).then_inc(sem("w2_ready"), 1)
            for w, first in ((w3_s, 2), (w4_s, 4)):
                for j in range(2):
                    chain(tt(prod[:, 0:KC, :], w[:, :, 0:DIM], rows[:, first + j:first + j + 1, :].to_broadcast([P, KC, DIM]), ALU.mult))
                    chain(nc.vector.tensor_reduce(w[:, :, DIM + j], prod[:, 0:KC, :], AX.X, ALU.add))
            dve.wait_ge(sem("pe_made"), T1_SUM)
            nc.vector.tensor_copy(t1_s[:, :, :].rearrange("p c n -> p (c n)"), ps[:, 1, :]).then_inc(sem("t1_ready"), 1)
            dve.wait_ge(sem("pe_made"), AB_SUM)
            nc.vector.tensor_copy(ab_s[:, :], ps[:, 2, 0:KC]).then_inc(sem("t1_ready"), 1)
            dve.wait_ge(sem("pe_made"), W2_SUM)
            nc.vector.scalar_tensor_tensor(out=b2_s[:, 0:DIM], in0=b2_s[:, 0:DIM], scalar=-3.0, in1=ps[:, 0, 0:DIM],
                                           op0=ALU.add, op1=ALU.subtract)
            nc.vector.tensor_scalar(b2_s[:, DIM:DIM + 2], ps[:, 0, DIM:DIM + 2], -1.0, None, ALU.mult)
            dve.wait_ge(sem("pe_made"), WL_TURNED)
            nc.vector.tensor_copy(wv_s[:, :, 0:DIM], ps[:, 3, :].rearrange("p (c n) -> p c n", c=KC))
            dve.wait_ge(sem("pe_made"), M_SUM)
            nc.vector.tensor_copy(m_s[:, :, :].rearrange("p c n -> p (c n)"), ps[:, 4, :])
            dve.wait_ge(sem("pe_made"), C_SUM)
            nc.vector.tensor_copy(c_s[:, :], ps[:, 5, 0:KC])
            nc.vector.tensor_copy(wv_s[:, :, DIM], ps[:, 5, KC:2 * KC])
            nc.vector.tensor_copy(bv_s[:, DIM:DIM + 1], ps[:, 5, 2 * KC:2 * KC + 1]).then_inc(sem("weights_ready"), 1)
            dve.wait_ge(sem("weights_ready"), 1)

            def statistics(k, p):
                if not live(p):
                    return
                if k == 0:
                    dve.wait_ge(sem(f"x_in{p.par}"), dma_count(p))
                else:
                    wait(dve, {1: "rsB", 2: "finC", 3: "finD"}[k], p)
                for g in range(G):
                    ins = nc.vector.bn_stats(stats[k][:, p.par, g, :], res[k][:, p.par, g, :])
                ins.then_inc(sem(f"stat{k}"), 1)

            def mean_and_variance(k, p):
                if not live(p):
                    return
                have(dve, p.n + 1)
                dve.wait_ge(sem("weights_ready"), 1)
                wait(dve, f"stat{k}", p)
                for g in range(G):
                    ins = nc.vector.bn_aggr(mv[k][:, p.par, g, :], stats[k][:, p.par, g, :])
                ins.then_inc(sem(f"mv{k}"), 1)
                wait(dve, f"mv{k}", p)
                nc.vector.tensor_scalar(nmean[k][:, p.par, :], mv[k][:, p.par, :, 0], -1.0, None, ALU.mult)
                nc.vector.tensor_scalar(vare[k][:, p.par, :], mv[k][:, p.par, :, 1], EPS, None, ALU.add)\
                    .then_inc(sem(f"aggr{k}"), 1)

            def make_masks(p):
                if not live(p):
                    return
                dve.wait_ge(sem(f"adj_in{p.par}"), dma_count(p))
                nc.vector.scalar_tensor_tensor(out=mask0[:, p.par, :, :], in0=adj_s[:, p.par, :, :], scalar=0.0,
                                               in1=offdiag[:, :].unsqueeze(1).to_broadcast([P, G, P]),
                                               op0=ALU.is_le, op1=ALU.mult)
                mine = masks[:, G * p.n:G * p.n + G, :] if isinstance(p.n, int) else masks[:, bass.ds(p.n * G, G), :]
                nc.vector.tensor_scalar(mine, adj_s[:, p.par, :, :], 0.0, NEG, ALU.is_equal, ALU.mult)\
                    .then_inc(sem("mk"), 1)

            def split_high(p):
                if not live(p):
                    return
                wait(dve, "as", p)
                src = ps[:, bank_of["as"], 0:G * NODES]
                nc.vector.tensor_copy(parts[:, p.par, :], src).then_inc(sem("sp0"), 1)
                wait(dve, "sp0", p)
                nc.vector.tensor_tensor(rest[MID:P, p.par, :], src[MID:P], parts[MID:P, p.par, :], ALU.subtract)\
                    .then_inc(sem("sp1"), 1)

            def split_low(p):
                if not live(p):
                    return
                wait(dve, "sp1", p)
                nc.vector.tensor_copy(parts[MID:P, p.par, :], rest[MID:P, p.par, :]).then_inc(sem("sp1b"), 1)
                wait(dve, "sp1b", p)
                nc.vector.tensor_tensor(parts[LO:P, p.par, :], rest[LO:P, p.par, :], parts[LO:P, p.par, :], ALU.subtract)\
                    .then_inc(sem("sp2"), 1)

            def bias_values0(g, p):
                if not live(p):
                    return
                wait(dve, f"xl{g}", p)
                tt(val0[g][:, p.par, :], ps[:, bank_of[f"xl{g}"], :], b1_s[:, :], ALU.add).then_inc(sem(f"xb{g}"), 1)

            def leaky0(g, p):
                if not live(p):
                    return
                wait(dve, f"az{g}", p)
                tt(attn0[g][:, p.par, :, :].rearrange("p h n -> p (h n)"), ps[:, bank_of[f"z{g}"], :], attn0[g][:, p.par, :, :].rearrange("p h n -> p (h n)"), ALU.max)\
                    .then_inc(sem(f"lk{g}"), 1)

            def maximum0(g, p):
                if not live(p):
                    return
                wait(dve, f"lk{g}", p)
                nc.vector.tensor_reduce(den0[g][:, p.par, :], attn0[g][:, p.par, :, :], AX.X, ALU.max).then_inc(sem(f"mxa{g}"), 1)
                wait(dve, f"mxa{g}", p)
                nc.vector.tensor_scalar(nmax0[g][:, p.par, :], den0[g][:, p.par, :], -1.0, None, ALU.mult).then_inc(sem(f"mx{g}"), 1)

            def reciprocal0(g, p):
                if not live(p):
                    return
                wait(dve, f"ex{g}", p)
                nc.vector.reciprocal(rden0[g][:, p.par, :], den0[g][:, p.par, :]).then_inc(sem(f"rd{g}"), 1)

            def elu0(g, p):
                if not live(p):
                    return
                wait(dve, f"el{g}", p)
                nc.vector.scalar_tensor_tensor(out=hid[g][:, p.par, :], in0=hid[g][:, p.par, :], scalar=1.0,
                                               in1=ps[:, bank_of[f"ot{g}"], :], op0=ALU.min, op1=ALU.max)\
                    .then_inc(sem(f"eu{g}"), 1)

            def bias_values(X, g, p):
                if not live(p):
                    return
                src, dst_sem, bias, n = {"B": (f"xm{g}", f"xn{g}", b2_s, DIM + 2), "C": (f"v{g}", f"vb{g}", bv_s, DIM + 1)}[X]
                wait(dve, src, p)
                tt(val[X][:, p.par, g, 0:n], ps[:, bank_of[src], 0:n], bias[:, :], ALU.add).then_inc(sem(dst_sem), 1)

            def leaky(X, p):
                if not live(p):
                    return
                wait(dve, f"az{X}", p)
                tt(prob[X][:, p.par, :], ps[:, bank_of[f"z{X}"], 0:G * NODES], prob[X][:, p.par, :], ALU.max).then_inc(sem(f"lk{X}"), 1)

            def maximum(X, p):
                if not live(p):
                    return
                if X == "C":
                    wait(dve, "sC", p)
                    src = ps[:, bank_of["sC"], 0:G * NODES]
                else:
                    wait(dve, f"lk{X}", p)
                    src = prob[X][:, p.par, :]
                nc.vector.tensor_reduce(mx[X][:, p.par, :], src.rearrange("p (g n) -> p g n", g=G), AX.X, ALU.max)\
                    .then_inc(sem(f"mxa{X}"), 1)
                wait(dve, f"mxa{X}", p)
                if X != "C":
                    nc.vector.tensor_scalar(nmax[X][:, p.par, :], mx[X][:, p.par, :], -1.0, None, ALU.mult).then_inc(sem(f"mx{X}"), 1)
                    return
                u = val[X][:, p.par, :, DIM]
                wait(dve, "vb0", p)
                wait(dve, "vb1", p)
                tt(mxu[:, p.par, :], mx[X][:, p.par, :], u, ALU.add).then_inc(sem("mxu"), 1)
                wait(dve, "mxu", p)
                tt(nmax[X][:, p.par, :], u, mxu[:, p.par, :], ALU.subtract).then_inc(sem("mxC"), 1)

            def reciprocal(X, p):
                if not live(p):
                    return
                wait(dve, f"ex{X}", p)
                nc.vector.reciprocal(rden[X][:, p.par, :], den[X][:, p.par, :]).then_inc(sem(f"rd{X}"), 1)

            def residual_b(p):
                if not live(p):
                    return
                wait(dve, "finC", p, back=2)
                wait(dve, "rdB", p)
                wait(dve, "oB", p)
                for g in range(G):
                    ins = nc.vector.scalar_tensor_tensor(out=res[1][:, p.par, g, :], in0=ps[:, bank_of["oB"], g * DIM:(g + 1) * DIM],
                                                         scalar=rden["B"][:, p.par, g:g + 1], in1=res[0][:, p.par, g, :],
                                                         op0=ALU.mult, op1=ALU.add)
                ins.then_inc(sem("rsB"), 1)

            def keep_top(g, p):
                if not live(p):
                    return
                src = graph_cols(prob["D"], p.par, g)
                first, second = (top[g][:, p.par, r, :] for r in range(TOPK_ROUNDS))
                rest_of = left[g][:, p.par, :]
                have(dve, p.n + 1, p.n * 3 + 1, p.n * 3 + 2, p.n * 3 + 3)
                dve.wait_ge(sem("weights_ready"), 1)
                wait(dve, "exD", p)
                nc.vector.max(first, src).then_inc(sem(f"top_{g}"), 1)
                dve.wait_ge(sem("weights_ready"), 1)
                dve.wait_ge(sem(f"top_{g}"), p.n * 3 + 1)
                nc.vector.match_replace(rest_of, first, src, -1.0).then_inc(sem(f"top_{g}"), 1)
                dve.wait_ge(sem("weights_ready"), 1)
                dve.wait_ge(sem(f"top_{g}"), p.n * 3 + 2)
                nc.vector.max(second, rest_of).then_inc(sem(f"top_{g}"), 1)
                dve.wait_ge(sem(f"top_{g}"), p.n * 3 + 3)
                nc.vector.scalar_tensor_tensor(out=graph_cols(kept, p.par, g), in0=src, scalar=second[:, 7:8], in1=src,
                                               op0=ALU.is_ge, op1=ALU.mult).then_inc(sem(f"tk{g}"), 1)

            def elu_sum(X, p):
                if not live(p):
                    return
                wait(dve, f"r{X}", p)
                nc.vector.scalar_tensor_tensor(out=elu[X][:, p.par, :], in0=elu[X][:, p.par, :], scalar=1.0,
                                               in1=pos[X][:, p.par, :], op0=ALU.min, op1=ALU.add).then_inc(sem(f"t{X}"), 1)

            def turn(t):
                statistics(0, lagged(t, 0))
                bias_values("C", 1, lagged(t, 2))
                reciprocal("D", lagged(t, 3))
                mean_and_variance(0, lagged(t, 0))
                bias_values("C", 0, lagged(t, 2))
                maximum("C", lagged(t, 2))
                reciprocal("E", lagged(t, 4))
                elu_sum("D", lagged(t, 3))
                elu0(0, lagged(t, 1))
                reciprocal("C", lagged(t, 2))
                statistics(3, lagged(t, 3))
                elu0(1, lagged(t, 1))
                mean_and_variance(3, lagged(t, 3))
                elu_sum("C", lagged(t, 2))
                bias_values("B", 0, lagged(t, 1))
                make_masks(lagged(t, 0))
                bias_values("B", 1, lagged(t, 1))
                statistics(2, lagged(t, 2))
                split_high(lagged(t, 0))
                mean_and_variance(2, lagged(t, 2))
                leaky("B", lagged(t, 1))
                maximum("B", lagged(t, 1))
                split_low(lagged(t, 0))
                bias_values0(1, lagged(t, 0))
                reciprocal("B", lagged(t, 1))
                leaky0(1, lagged(t, 0))
                maximum0(1, lagged(t, 0))
                residual_b(lagged(t, 1))
                statistics(1, lagged(t, 1))
                mean_and_variance(1, lagged(t, 1))
                leaky0(0, lagged(t, 0))
                maximum0(0, lagged(t, 0))
                reciprocal0(1, lagged(t, 0))
                leaky("D", lagged(t, 2))
                maximum("D", lagged(t, 2))
                reciprocal0(0, lagged(t, 0))
                bias_values0(0, lagged(t, 0))
                elu_sum("E", lagged(t, 4))
                keep_top(0, lagged(t, 2))
                keep_top(1, lagged(t, 2))
                leaky("E", lagged(t, 3))
                maximum("E", lagged(t, 3))

            over_turns(dve, turn)


_INS = ['x', 'adj', 'L0_gnn_W1', 'L0_gnn_att_src1', 'L0_gnn_att_dst1', 'L0_gnn_b1', 'L0_gnn_W2', 'L0_gnn_att_src2',
        'L0_gnn_att_dst2', 'L0_gnn_b2', 'L1_gnn_W', 'L1_gnn_b', 'L1_gnn_attn', 'L2_gnn_W', 'L2_gnn_a', 'L3_gnn_w',
        'L3_gnn_a1', 'L3_gnn_a2']


def kernel(**inputs):
    import concourse.bacc as bacc
    from concourse.bass_utils import run_bass_kernel_spmd

    nc = bacc.Bacc("TRN2", target_bir_lowering=False, num_devices=1)
    arrays, args = {}, []
    for name in _INS:
        a = np.ascontiguousarray(inputs[name])
        arrays[f"in_{name}"] = a
        args.append(nc.dram_tensor(f"in_{name}", a.shape, mybir.dt.from_np(a.dtype), kind="ExternalInput").ap())
    out = nc.dram_tensor("out", (GRAPHS, NODES, DIM), F32, kind="ExternalOutput").ap()
    graph_layers(nc, *args, out)
    return run_bass_kernel_spmd(nc, [arrays], core_ids=[0]).results[0]["out"]
```

```python
from collections import namedtuple
from contextlib import ExitStack

import numpy as np

import concourse.bass as bass
import concourse.mybir as mybir

F32 = mybir.dt.float32
F32R = mybir.dt.float32r
BF16 = mybir.dt.bfloat16
I32 = mybir.dt.int32
ALU = mybir.AluOpType
ACT = mybir.ActivationFunctionType
AX = mybir.AxisListType

GRAPHS, NODES, DIM = 64, 128, 256
P = 128
G = 2
PAIRS = GRAPHS // G
KC = DIM // P
HEADS, HF = 4, 128
HID = HEADS * HF
NEG = -1e30
LOWEST = -3e38
EPS = 1e-5
SLOPE_L0, SLOPE_L2, SLOPE_L3 = 0.2, 0.2, 0.1
TOPK_ROUNDS = 2
BANKS = 8
HIGH, LOW = 0, 1
HI, MID, LO = 0, 64, 96

LOOP_FROM = 8
LAST_LAG = 7
STORE_LAG = 7
W1_LOADS = 4
WEIGHT_LOADS = 14

SECOND_HALF = {**{f"nv{k}": f"aggr{k}" for k in range(4)}, **{f"ng{X}": f"mx{X}" for X in "01BDE"}}

Pair = namedtuple("Pair", "n par")


def lagged(turn, lag):
    return Pair(turn.n - lag, (turn.par - lag) % 2)


def live(p):
    return not isinstance(p.n, int) or 0 <= p.n < PAIRS


def graph_layers(nc, x, adj, w1, src1, dst1, b1, w2, src2, dst2, b2, wl, bl, al, w3, a3, w4, a4src, a4dst, out):
    with ExitStack() as ctx:
        def sb(name, shape, dt=F32):
            return ctx.enter_context(nc.sbuf_tensor(name, shape, dt))

        def two(name, shape, dt=F32):
            return sb(name, [P, 2, *shape], dt)

        sems = {}

        def sem(name):
            if name not in sems:
                sems[name] = ctx.enter_context(nc.semaphore(name))
            return sems[name]

        def wait(eng, name, p, back=0):
            n = p.n + 1 - back
            if isinstance(n, int):
                n = min(n, PAIRS)
                if n < 1:
                    return
            if name in SECOND_HALF:
                eng.wait_ge(sem(SECOND_HALF[name]), n * 2)
            else:
                eng.wait_ge(sem(name), n * 2 - 1 if name in SECOND_HALF.values() else n)

        def have(eng, *values):
            for v in values:
                if not isinstance(v, int):
                    eng.compute_val(v)

        ident = sb("ident", [P, P])
        ident_bf = sb("ident_bf", [P, P], BF16)
        ones = sb("ones", [P, P])
        offdiag = sb("offdiag", [P, P])
        pick_src = sb("pick_src", [P, HEADS, P], BF16)
        pick_dst = sb("pick_dst", [P, HEADS, P], BF16)
        minus1 = sb("minus1", [P, 1])
        minus_half = sb("minus_half", [P, G])
        w1_s = sb("w1_s", [P, 2, KC, HID], F32R)
        coef_s = sb("coef_s", [P, 2, KC, P], F32R)
        b1_s = sb("b1_s", [P, HID])
        w2_s = sb("w2_s", [P, 2, HEADS, DIM + 2], F32R)
        b2_s = sb("b2_s", [P, DIM + 2])
        bl_col = sb("bl_col", [P, KC])
        ab_s = sb("ab_s", [P, KC])
        m_s = sb("m_s", [P, 2, KC, DIM], F32R)
        c_s = sb("c_s", [P, 2 * KC])
        wv_s = sb("wv_s", [P, 2, KC, DIM + 2], F32R)
        bv_s = sb("bv_s", [P, DIM + 1])
        w3_s = sb("w3_s", [P, 2, KC, DIM + 2], F32R)
        w4_s = sb("w4_s", [P, 2, KC, DIM + 2], F32R)
        mask0 = two("mask0", [G, NODES], BF16)
        masks = sb("masks", [P, GRAPHS, NODES], BF16)
        adj_s = two("adj_s", [G, NODES], I32)
        res = [two(f"res{k}", [G, DIM]) for k in range(5)]
        stats = [two(f"stats{k}", [G, 6]) for k in range(4)]
        mv = [two(f"mv{k}", [G, 2]) for k in range(4)]
        nmean = [two(f"nmean{k}", [G]) for k in range(4)]
        vare = [two(f"vare{k}", [G]) for k in range(4)]
        rstd = [two(f"rstd{k}", [G]) for k in range(4)]
        norm = [sb(f"norm{k}", [P, G, DIM]) for k in range(4)]
        hT = [sb(f"hT{k}", [P, 2, KC, G * NODES], F32R) for k in range(4)]
        hT1 = two("hT1_whole", [KC, G * NODES])
        parts = two("parts", [G * NODES], BF16)
        rest = two("rest", [G * NODES])
        val0_all = sb("val0", [P, G, 2, HID])
        val0 = [val0_all[:, g, :, :] for g in range(G)]
        attn0_all = sb("attn0", [P, G, 2, HEADS, NODES])
        attn0 = [attn0_all[:, g, :, :, :] for g in range(G)]
        nmax0 = [two(f"nmax0_{g}", [HEADS]) for g in range(G)]
        den0 = [two(f"den0_{g}", [HEADS]) for g in range(G)]
        rden0 = [two(f"rden0_{g}", [HEADS]) for g in range(G)]
        attnT0 = [sb(f"attnT0_{g}", [P, HEADS, NODES]) for g in range(G)]
        hid_all = sb("hid", [P, G, 2, HID])
        hid = [hid_all[:, g, :, :] for g in range(G)]
        hid_r = [sb(f"hid_r{g}", [P, 2, HID], F32R) for g in range(G)]
        val = {X: two(f"val{X}", [G, DIM + 2]) for X in "BCDE"}
        nmax = {X: two(f"nmax{X}", [G]) for X in "BCDE"}
        mxu = two("mxu", [G])
        mx = {X: two(f"mx{X}", [G]) for X in "BCDE"}
        den = {X: two(f"den{X}", [G]) for X in "BCDE"}
        rden = {X: two(f"rden{X}", [G]) for X in "BCDE"}
        prob = {X: two(f"prob{X}", [G * NODES]) for X in "BCDE"}
        probT = {X: sb(f"probT{X}", [P, G * NODES]) for X in "BCDE"}
        qT = sb("qT", [P, KC, G * NODES])
        top = [two(f"top_{g}", [TOPK_ROUNDS, 8]) for g in range(G)]
        left = [two(f"left_{g}", [NODES]) for g in range(G)]
        kept = two("kept", [G * NODES])
        pos = {X: sb(f"pos{X}", [P, G * DIM]) for X in "CDE"}
        elu = {X: two(f"elu{X}", [G * DIM]) for X in "CDE"}

        ps = ctx.enter_context(nc.psum_tensor("ps", [P, BANKS, 512], F32))

        def place(home, start, shape):
            n = int(np.prod(shape))
            if len(home.shape) == 4:
                whole = home[:, :, :, :].rearrange("p a g n -> p (a g n)")
            else:
                whole = home[:, :, :].rearrange("p a n -> p (a n)")
            return whole[:, start:start + n].rearrange("p (c n) -> p c n", c=shape[0])

        w1_in = place(res[4], 0, [KC, HID])
        rows1 = place(elu["E"], 0, [2, HID])
        w2_in = place(val["E"], 0, [HEADS, DIM + 2])
        wl_in = place(elu["D"], 0, [KC, DIM])
        al_in = place(elu["D"], KC * DIM, [KC, DIM])
        t1_s = place(elu["C"], 0, [KC, DIM])
        coef_in = place(elu["C"], KC * DIM, [KC, P])
        w3_in = place(val["D"], 0, [KC, DIM + 2])
        w4_in = place(val["D"], KC * (DIM + 2), [KC, DIM + 2])
        rows2 = place(res[2], 0, [2, DIM])
        rows34 = place(res[3], 0, [4, DIM])
        prod1 = attnT0[0][:, :, :].rearrange("p h n -> p (h n)")
        prod2 = [place(hid_all, j * HEADS * DIM, [HEADS, DIM]) for j in range(2)]
        prod3 = [place(val["B"], j * KC * DIM, [KC, DIM]) for j in range(2)]
        prod4 = [place(val["C"], j * KC * DIM, [KC, DIM]) for j in range(2)]

        bank_of = {"ptE": 0, "tr3": 1, "z1": 2, "ptD": 3, "z0": 4, "oE": 5, "wE1": 6, "ptB": 0, "wE0": 1, "oB": 2, "xl1": 3, "xl0": 4, "tr2": 5, "pt1": 6, "oD": 0, "zE": 1, "tr1": 2, "ot1": 3, "pt0": 4, "wD0": 5, "wD1": 6, "ot0": 0, "gt": 1, "v0": 2, "v1": 3, "sC": 4, "tr0": 5, "zD": 6, "xm1": 0, "as": 1, "ptC": 2, "xm0": 3, "oC": 4, "zB": 5}
        made_in = {"w2_sum": 0, "t1": 2, "ab": 3, "wl_turned": 4, "m": 6, "c": 7}

        x_v = x.rearrange("(q g) n f -> q n g f", g=G)
        adj_v = adj.rearrange("(q g) m n -> q m g n", g=G)
        out_v = out.rearrange("(q g) n f -> q n g f", g=G)
        def rise(slope):
            return (1 - slope) / slope

        def flat2(ap):
            return ap.rearrange("p c n -> p (c n)")

        SLOPE = {"B": SLOPE_L0, "D": SLOPE_L2, "E": SLOPE_L3}
        ROW = {"B": DIM + 1, "D": DIM, "E": DIM}
        COL = {"B": DIM, "D": DIM + 1, "E": DIM + 1}
        LAYER = {"C": 1, "D": 2, "E": 3}

        def graph_cols(tile, par, g, n=NODES):
            return tile[:, par, g * n:(g + 1) * n]

        T1_SUM, AB_SUM, WL_TURNED, M_SUM, C_SUM, W2_SUM = range(1, 7)

        block = ctx.enter_context(nc.Block())

        def over_turns(eng, turn, after_first=None):
            for t in range(LOOP_FROM):
                turn(Pair(t, t % 2))
                if t == 0 and after_first:
                    after_first()
            with eng.Fori(LOOP_FROM // 2, PAIRS // 2) as i:
                turn(Pair(i * 2, 0))
                turn(Pair(i * 2 + 1, 1))
            for t in range(PAIRS, PAIRS + LAST_LAG):
                turn(Pair(t, t % 2))

        def on_all(v, n):
            return v.rearrange("(a n) -> a n", a=1).to_broadcast([P, n])

        @block.sync
        def _(sp):
            def of_pair(view, p):
                if isinstance(p.n, int):
                    return view[p.n]
                return view[bass.ds(p.n, 1)].rearrange("a n g f -> (a n) g f")

            def load_pair(p):
                if not live(p):
                    return
                wait(sp, "rsB", p, back=2)
                sp.dma_start(res[0][:, p.par, :, :], of_pair(x_v, p))\
                    .then_inc(sem(f"x_in{p.par}"), 16)
                wait(sp, "mk", p, back=2)
                sp.dma_start(adj_s[:, p.par, :, :], of_pair(adj_v, p))\
                    .then_inc(sem(f"adj_in{p.par}"), 16)

            def store_pair(p):
                if not live(p):
                    return
                wait(sp, "finE", p)
                sp.dma_start(of_pair(out_v, p), res[4][:, p.par, :, :])\
                    .then_inc(sem(f"stored{p.par}"), 16)

            def turn(t):
                done = lagged(t, STORE_LAG)
                have(sp, t.n - 1, done.n + 1)
                load_pair(t)
                store_pair(done)

            over_turns(sp, turn)
            for par in range(2):
                sp.wait_ge(sem(f"stored{par}"), 16 * (PAIRS // 2))

        def dma_count(p):
            n = p.n - p.par
            return 16 * (n // 2 + 1) if isinstance(n, int) else n * 8 + 16

        @block.gpsimd
        def _(pool):
            made = sem("pool_made")
            steps = [0]

            def chain(ins):
                steps[0] += 1
                ins.then_inc(made, 1)
                pool.wait_ge(made, steps[0])

            def diagonal(tile, fill, pattern, offset):
                chain(nc.gpsimd.affine_select(out=tile, in_=tile, compare_op=ALU.not_equal, fill=fill, base=-offset,
                                              pattern=pattern, channel_multiplier=1))

            for tile, value in ((ident, 0.0), (ident_bf, 0.0), (ones, 1.0), (offdiag, NEG), (pick_src, 0.0),
                                (pick_dst, 0.0), (minus_half, -0.5)):
                whole = tile[:, :] if len(tile.shape) == 2 else tile[:, :, :]
                chain(nc.gpsimd.memset(whole, value))
            diagonal(ident[:, :], 1.0, [[-1, P]], 0)
            diagonal(ident_bf[:, :], 1.0, [[-1, P]], 0)
            diagonal(offdiag[:, :], 0.0, [[-1, P]], 0)
            for start in (HI, MID, LO):
                diagonal(pick_src[:, :, :], 1.0, [[-1, HEADS], [0, P]], start)
                diagonal(pick_dst[:, :, :], 1.0, [[-1, HEADS], [0, P]], start + HEADS)
            nc.gpsimd.memset(minus1[:, :], -1.0).then_inc(sem("constants"), 1)

            def later_weights():
                pool.wait_ge(sem("weights_in"), 16 * WEIGHT_LOADS)
                for w_in, prods, vectors, chunks in ((w2_in, prod2, rows2, HEADS), (w3_in, prod3, rows34[:, 0:2, :], KC),
                                                     (w4_in, prod4, rows34[:, 2:4, :], KC)):
                    for j in range(2):
                        nc.gpsimd.tensor_tensor(prods[j], w_in[:, :, 0:DIM], vectors[:, j:j + 1, :].to_broadcast([P, chunks, DIM]),
                                                ALU.mult).then_inc(sem("multiplied"), 1)
                for i, (w, w_in) in enumerate(((w2_s, w2_in), (w3_s, w3_in), (w4_s, w4_in))):
                    pool.wait_ge(sem("weights_high"), i + 1)
                    ins = nc.gpsimd.tensor_tensor(w[:, LOW, :, :], w_in, w[:, HIGH, :, :].bitcast(F32), ALU.subtract)
                ins.then_inc(sem("weights_ready"), 1)
                pool.wait_ge(sem("weights_ready"), 2)

            def reciprocal_std(k, p):
                if not live(p):
                    return
                wait(pool, f"nv{k}", p)
                nc.gpsimd.tensor_tensor(rstd[k][:, p.par, :], vare[k][:, p.par, :], minus_half[:, :], ALU.pow)\
                    .then_inc(sem(f"pow{k}"), 1)

            def normalise(k, p):
                if not live(p):
                    return
                have(pool, p.n, p.n + 1)
                pool.wait_ge(sem("constants"), 1)
                wait(pool, f"tr{k}", p, back=1)
                wait(pool, f"pow{k}", p)
                for g in range(G):
                    ins = nc.gpsimd.tensor_scalar(norm[k][:, g, :], res[k][:, p.par, g, :],
                                                  nmean[k][:, p.par, g:g + 1], rstd[k][:, p.par, g:g + 1],
                                                  ALU.add, ALU.mult)
                ins.then_inc(sem(f"norm{k}"), 1)

            def attention_weights(g, p):
                if not live(p):
                    return
                wait(pool, f"rd{g}", p)
                nc.gpsimd.tensor_tensor(attn0[g][:, p.par, :, :], attn0[g][:, p.par, :, :],
                                        rden0[g][:, p.par, :].unsqueeze(2).to_broadcast([P, HEADS, NODES]),
                                        ALU.mult).then_inc(sem(f"nr{g}"), 1)

            def low_h1(p):
                if not live(p):
                    return
                wait(pool, "v1", p, back=1)
                wait(pool, "hi1", p)
                nc.gpsimd.tensor_tensor(flat2(hT[1][:, LOW, :, :]), flat2(hT1[:, p.par, :, :]),
                                        flat2(hT[1][:, HIGH, :, :]).bitcast(F32), ALU.subtract).then_inc(sem("lo1"), 1)

            def low_hid(g, p):
                if not live(p):
                    return
                wait(pool, f"xm{g}", p, back=1)
                wait(pool, f"hh{g}", p)
                nc.gpsimd.tensor_tensor(hid_r[g][:, LOW, :], hid[g][:, p.par, :], hid_r[g][:, HIGH, :].bitcast(F32),
                                        ALU.subtract).then_inc(sem(f"hl{g}"), 1)

            def negative_maximum_c(p):
                if not live(p):
                    return
                u = val["C"][:, p.par, :, DIM]
                wait(pool, "mxC", p)
                wait(pool, "vb0", p)
                wait(pool, "vb1", p)
                nc.gpsimd.tensor_tensor(mxu[:, p.par, :], mx["C"][:, p.par, :], u, ALU.add).then_inc(sem("mxu"), 1)
                wait(pool, "mxu", p)
                nc.gpsimd.tensor_tensor(nmax["C"][:, p.par, :], u, mxu[:, p.par, :], ALU.subtract).then_inc(sem("ngC"), 1)

            def add_residual(X, p):
                if not live(p):
                    return
                k = LAYER[X]
                wait(pool, f"t{X}", p)
                if X != "E":
                    wait(pool, {"C": "finD", "D": "finE"}[X], p, back=2)
                if X == "E" and not (isinstance(p.n, int) and p.n < 2):
                    pool.wait_ge(sem(f"stored{p.par}"), dma_count(p) - 16)
                nc.gpsimd.tensor_tensor(res[k + 1][:, p.par, :, :].rearrange("p g f -> p (g f)"),
                                        res[k][:, p.par, :, :].rearrange("p g f -> p (g f)"),
                                        elu[X][:, p.par, :], ALU.add).then_inc(sem(f"fin{X}"), 1)

            def turn(t):
                normalise(3, lagged(t, 5))
                add_residual("C", lagged(t, 3))
                reciprocal_std(2, lagged(t, 3))
                normalise(2, lagged(t, 3))
                attention_weights(1, lagged(t, 1))
                reciprocal_std(1, lagged(t, 2))
                normalise(1, lagged(t, 2))
                attention_weights(0, lagged(t, 1))
                add_residual("E", lagged(t, 6))
                low_h1(lagged(t, 2))
                add_residual("D", lagged(t, 4))
                reciprocal_std(0, lagged(t, 0))
                normalise(0, lagged(t, 0))
                low_hid(1, lagged(t, 1))
                negative_maximum_c(lagged(t, 2))
                low_hid(0, lagged(t, 1))
                reciprocal_std(3, lagged(t, 4))

            over_turns(pool, turn, later_weights)

        @block.tensor
        def _(pe):
            def mm(out_, lhsT, rhs, start, stop):
                return nc.tensor.matmul(out_, lhsT, rhs, start=start, stop=stop)

            def mm_split(out_, factors):
                passes = [(lhsT(a), rhs(b)) for lhsT, rhs in factors for a, b in ((HIGH, HIGH), (HIGH, LOW), (LOW, HIGH))]
                for i, (a, b) in enumerate(passes):
                    ins = mm(out_, a, b, i == 0, i == len(passes) - 1)
                return ins

            pe.wait_ge(sem("constants"), 1)

            def later_weights():
                pe.wait_ge(sem("weights_in"), 16 * WEIGHT_LOADS)
                for jc in range(KC):
                    for oc in range(KC):
                        ins = mm(ps[:, made_in["t1"], jc * DIM:(jc + 1) * DIM], al_in[:, oc, jc * P:(jc + 1) * P], wl_in[:, oc, :],
                                 oc == 0, oc == KC - 1)
                ins.then_inc(sem("pe_made"), 1)
                for jc in range(KC):
                    for oc in range(KC):
                        ins = mm(ps[:, made_in["ab"], jc:jc + 1], al_in[:, oc, jc * P:(jc + 1) * P], bl_col[:, oc:oc + 1],
                                 oc == 0, oc == KC - 1)
                ins.then_inc(sem("pe_made"), 1)
                for ic in range(KC):
                    for oc in range(KC):
                        ins = nc.tensor.transpose(ps[:, made_in["wl_turned"], (ic * KC + oc) * P:(ic * KC + oc + 1) * P],
                                                  wl_in[:, oc, ic * P:(ic + 1) * P], ident[:, :])
                ins.then_inc(sem("pe_made"), 1)
                pe.wait_ge(sem("t1_ready"), 2)
                for ic in range(KC):
                    for jc in range(KC):
                        ins = mm(ps[:, made_in["m"], ic * DIM:(ic + 1) * DIM], t1_s[:, jc, ic * P:(ic + 1) * P], wl_in[:, jc, :],
                                 jc == 0, jc == KC - 1)
                ins.then_inc(sem("pe_made"), 1)
                for ic in range(KC):
                    for jc in range(KC):
                        mm(ps[:, made_in["c"], ic:ic + 1], wl_in[:, jc, ic * P:(ic + 1) * P], ab_s[:, jc:jc + 1], jc == 0, jc == KC - 1)
                for ic in range(KC):
                    for jc in range(KC):
                        mm(ps[:, made_in["c"], KC + ic:KC + ic + 1], t1_s[:, jc, ic * P:(ic + 1) * P], bl_col[:, jc:jc + 1],
                           jc == 0, jc == KC - 1)
                for jc in range(KC):
                    ins = mm(ps[:, made_in["c"], 2 * KC:2 * KC + 1], ab_s[:, jc:jc + 1].to_broadcast([P, P]), bl_col[:, jc:jc + 1],
                             jc == 0, jc == KC - 1)
                ins.then_inc(sem("pe_made"), 1)
                for h in range(HEADS):
                    if h == 0:
                        pe.wait_ge(sem("columns_made"), 1)
                    ins = mm(ps[:, made_in["w2_sum"], 0:DIM + 2], ones[:, :], w2_in[:, h, :], h == 0, h == HEADS - 1)
                ins.then_inc(sem("pe_made"), 1)
                pe.wait_ge(sem("weights_ready"), 2)

            def bank_free(p, bank, after):
                name, turn, lag = after
                wait(pe, name, lagged(turn, lag))

            def turn_norm(k, p, bank, after):
                if not live(p):
                    return
                bank_free(p, bank, after)
                wait(pe, f"norm{k}", p)
                for c in range(KC):
                    for g in range(G):
                        ins = nc.tensor.transpose(ps[:, bank, (c * G + g) * P:(c * G + g + 1) * P],
                                                  norm[k][:, g, c * P:(c + 1) * P], ident[:, :])
                ins.then_inc(sem(f"tr{k}"), 1)

            def w1_ready(p):
                if isinstance(p.n, int) and p.n == 0:
                    pe.wait_ge(sem("w1_ready"), 1)

            def coefficients(p, bank, after):
                if not live(p):
                    return
                bank_free(p, bank, after)
                w1_ready(p)
                wait(pe, "lo0", p)
                mm_split(ps[:, bank, 0:G * NODES],
                         [(lambda part, c=c: coef_s[:, part, c, :], lambda part, c=c: hT[0][:, part, c, :])
                          for c in range(KC)]).then_inc(sem("as"), 1)

            def features_times(k, g, w, out_):
                return mm_split(out_, [(lambda part, c=c: hT[k][:, part, c, g * P:(g + 1) * P],
                                        lambda part, c=c: w[:, part, c, :]) for c in range(KC)])

            def values0(g, p, bank, after):
                if not live(p):
                    return
                bank_free(p, bank, after)
                w1_ready(p)
                wait(pe, "lo0", p)
                features_times(0, g, w1_s, ps[:, bank, :]).then_inc(sem(f"xl{g}"), 1)

            def scores0(g, p, bank, after):
                if not live(p):
                    return
                bank_free(p, bank, after)
                wait(pe, "mk", p)
                wait(pe, "sp2", p)
                mm(ps[:, bank, :], mask0[:, p.par, g, :], ident_bf[:, :].unsqueeze(1).to_broadcast([P, HEADS, P]), True, False)
                mine = graph_cols(parts, p.par, g)
                mm(ps[:, bank, :], mine, pick_dst[:, :, :], False, False)
                for h in range(HEADS):
                    ins = mm(ps[:, bank, h * P:(h + 1) * P], pick_src[:, h, :], mine, False, h == HEADS - 1)
                ins.then_inc(sem(f"z{g}"), 1)

            def turn_weights0(g, p, bank, after):
                if not live(p):
                    return
                bank_free(p, bank, after)
                wait(pe, f"nr{g}", p)
                for h in range(HEADS):
                    ins = nc.tensor.transpose(ps[:, bank, h * P:(h + 1) * P], attn0[g][:, p.par, h, :], ident[:, :])
                ins.then_inc(sem(f"pt{g}"), 1)

            def attend0(g, p, bank, after):
                if not live(p):
                    return
                bank_free(p, bank, after)
                wait(pe, f"xb{g}", p)
                wait(pe, f"pc{g}", p)
                for h in range(HEADS):
                    ins = mm(ps[:, bank, h * P:(h + 1) * P], val0[g][:, p.par, h * HF:(h + 1) * HF],
                             attnT0[g][:, h, :], True, True)
                ins.then_inc(sem(f"ot{g}"), 1)

            def values_b(g, p, bank, after):
                if not live(p):
                    return
                bank_free(p, bank, after)
                wait(pe, f"hl{g}", p)
                mm_split(ps[:, bank, 0:DIM + 2],
                         [(lambda part, h=h: hid_r[g][:, part, h * P:(h + 1) * P], lambda part, h=h: w2_s[:, part, h, :])
                          for h in range(HEADS)]).then_inc(sem(f"xm{g}"), 1)

            def values(X, g, p, bank, after):
                if not live(p):
                    return
                w = w3_s if X == "D" else w4_s
                k = LAYER[X]
                bank_free(p, bank, after)
                wait(pe, f"lo{k}", p)
                features_times(k, g, w, ps[:, bank, 0:DIM + 2]).then_inc(sem(f"w{X}{g}"), 1)

            def scores(X, p, bank, after):
                if not live(p):
                    return
                bank_free(p, bank, after)
                copied = ("xn0", "xn1") if X == "B" else (f"wc{X}0", f"wc{X}1")
                for name in copied:
                    wait(pe, name, p)
                for g in range(G):
                    dst = ps[:, bank, g * P:(g + 1) * P]
                    if X == "B":
                        mm(dst, mask0[:, p.par, g, :], ident_bf[:, :], True, False)
                    else:
                        mm(dst, ident_bf[:, :], graph_mask(p, g), True, False)
                    col = val[X][:, p.par, g, COL[X]:COL[X] + 1]
                    ins = mm(dst, col.to_broadcast([P, P]), ident[:, :], False, True)
                ins.then_inc(sem(f"z{X}"), 1)

            def graph_mask(p, g):
                if isinstance(p.n, int):
                    return masks[:, G * p.n + g, :]
                return masks[:, bass.ds(p.n * G + g, 1), :].rearrange("p a n -> p (a n)")

            def turn_weights(X, p, bank, after):
                if not live(p):
                    return
                bank_free(p, bank, after)
                src, name = (kept, "tk") if X == "D" else (prob[X], f"ex{X}")
                wait(pe, name, p)
                for g in range(G):
                    ins = nc.tensor.transpose(ps[:, bank, g * P:(g + 1) * P], graph_cols(src, p.par, g), ident[:, :])
                ins.then_inc(sem(f"pt{X}"), 1)

            def attend(X, p, bank, after):
                if not live(p):
                    return
                bank_free(p, bank, after)
                wait(pe, f"pc{X}", p)
                for g in range(G):
                    ins = mm(ps[:, bank, g * DIM:(g + 1) * DIM], probT[X][:, g * P:(g + 1) * P],
                             val[X][:, p.par, g, 0:DIM], True, True)
                ins.then_inc(sem(f"o{X}"), 1)

            def queries(p, bank, after):
                if not live(p):
                    return
                bank_free(p, bank, after)
                wait(pe, "lo1", p)
                for ic in range(KC):
                    ins = mm_split(ps[:, bank, ic * G * P:(ic + 1) * G * P],
                                   [(lambda part, c=c: m_s[:, part, c, ic * P:(ic + 1) * P],
                                     lambda part, c=c: hT[1][:, part, c, :]) for c in range(KC)])
                ins.then_inc(sem("gt"), 1)

            def values_c(g, p, bank, after):
                if not live(p):
                    return
                bank_free(p, bank, after)
                wait(pe, "lo1", p)
                features_times(1, g, wv_s, ps[:, bank, 0:DIM + 2]).then_inc(sem(f"v{g}"), 1)

            def scores_c(p, bank, after):
                if not live(p):
                    return
                bank_free(p, bank, after)
                wait(pe, "gc", p)
                for g in range(G):
                    dst = ps[:, bank, g * P:(g + 1) * P]
                    mm(dst, ident_bf[:, :], graph_mask(p, g), True, False)
                    for c in range(KC):
                        ins = mm(dst, qT[:, c, g * P:(g + 1) * P], hT1[:, p.par, c, g * P:(g + 1) * P],
                                 False, c == KC - 1)
                ins.then_inc(sem("sC"), 1)

            def turn(t):
                turn_weights("E", lagged(t, 6), bank=bank_of["ptE"], after=("xn1", t, 2))
                turn_norm(3, lagged(t, 5), bank=bank_of["tr3"], after=("sp1", t, 1))
                scores0(1, lagged(t, 1), bank=bank_of["z1"], after=("pcC", t, 3))
                turn_weights("D", lagged(t, 4), bank=bank_of["ptD"], after=("xn0", t, 2))
                scores0(0, lagged(t, 1), bank=bank_of["z0"], after=("rC", t, 3))
                attend("E", lagged(t, 6), bank=bank_of["oE"], after=("mxB", t, 2))
                values("E", 1, lagged(t, 5), bank=bank_of["wE1"], after=("mxD", t, 4))
                turn_weights("B", lagged(t, 2), bank=bank_of["ptB"], after=("pcE", t, 6))
                values("E", 0, lagged(t, 5), bank=bank_of["wE0"], after=("lo3", t, 5))
                attend("B", lagged(t, 2), bank=bank_of["oB"], after=("mx1", t, 1))
                values0(1, lagged(t, 1), bank=bank_of["xl1"], after=("pcD", t, 4))
                values0(0, lagged(t, 1), bank=bank_of["xl0"], after=("mx0", t, 1))
                turn_norm(2, lagged(t, 3), bank=bank_of["tr2"], after=("rE", t, 6))
                turn_weights0(1, lagged(t, 1), bank=bank_of["pt1"], after=("wcE1", t, 5))
                attend("D", lagged(t, 4), bank=bank_of["oD"], after=("pcB", t, 2))
                scores("E", lagged(t, 5), bank=bank_of["zE"], after=("wcE0", t, 5))
                turn_norm(1, lagged(t, 2), bank=bank_of["tr1"], after=("rsB", t, 2))
                attend0(1, lagged(t, 1), bank=bank_of["ot1"], after=("xb1", t, 1))
                turn_weights0(0, lagged(t, 1), bank=bank_of["pt0"], after=("xb0", t, 1))
                values("D", 0, lagged(t, 3), bank=bank_of["wD0"], after=("lo2", t, 3))
                values("D", 1, lagged(t, 3), bank=bank_of["wD1"], after=("pc1", t, 1))
                attend0(0, lagged(t, 1), bank=bank_of["ot0"], after=("rD", t, 4))
                queries(lagged(t, 2), bank=bank_of["gt"], after=("mxE", t, 5))
                values_c(0, lagged(t, 2), bank=bank_of["v0"], after=("rl1", t, 2))
                values_c(1, lagged(t, 2), bank=bank_of["v1"], after=("eu1", t, 1))
                scores_c(lagged(t, 2), bank=bank_of["sC"], after=("pc0", t, 1))
                turn_norm(0, lagged(t, 0), bank=bank_of["tr0"], after=("wcD0", t, 3))
                scores("D", lagged(t, 3), bank=bank_of["zD"], after=("wcD1", t, 3))
                values_b(1, lagged(t, 1), bank=bank_of["xm1"], after=("eu0", t, 1))
                coefficients(lagged(t, 0), bank=bank_of["as"], after=("gc", t, 2))
                turn_weights("C", lagged(t, 2), bank=bank_of["ptC"], after=("vb0", t, 2))
                values_b(0, lagged(t, 1), bank=bank_of["xm0"], after=("vb1", t, 2))
                attend("C", lagged(t, 2), bank=bank_of["oC"], after=("exC", t, 2))
                scores("B", lagged(t, 1), bank=bank_of["zB"], after=("lo0", t, 0))

            over_turns(pe, turn, later_weights)

        @block.scalar
        def _(act):
            def relu_copy(k, p):
                if not live(p):
                    return
                if k == 0:
                    wait(act, "xl0", p, back=1)
                if k == 2:
                    wait(act, "wD1", p, back=1)
                if k == 3:
                    wait(act, "wE0", p, back=1)
                if k == 1:
                    wait(act, "sC", p, back=2)
                wait(act, f"tr{k}", p)
                dst = hT1[:, p.par, :, :] if k == 1 else hT[k][:, HIGH, :, :]
                nc.scalar.activation(flat2(dst), ps[:, bank_of[f"tr{k}"], :],
                                     ACT.Relu).then_inc(sem(f"rl{k}"), 1)

            def split_high(p):
                if not live(p):
                    return
                wait(act, "z0", p, back=2)
                wait(act, "z1", p, back=2)
                wait(act, "as", p)
                nc.scalar.activation(parts[:, p.par, :], ps[:, bank_of["as"], 0:G * NODES], ACT.Copy).then_inc(sem("sp0"), 1)

            def split_middle(p):
                if not live(p):
                    return
                wait(act, "sp1", p)
                nc.scalar.activation(parts[MID:P, p.par, :], rest[MID:P, p.par, :], ACT.Copy).then_inc(sem("sp1b"), 1)

            def scaled0(g, p):
                if not live(p):
                    return
                wait(act, f"pt{g}", p, back=2)
                wait(act, f"z{g}", p)
                nc.scalar.activation(flat2(attn0[g][:, p.par, :, :]), ps[:, bank_of[f"z{g}"], :], ACT.Relu, scale=rise(SLOPE_L0))\
                    .then_inc(sem(f"az{g}"), 1)

            def exponentials0(g, p):
                if not live(p):
                    return
                wait(act, f"ng{g}", p)
                for h in range(HEADS):
                    ins = nc.scalar.activation(attn0[g][:, p.par, h, :], attn0[g][:, p.par, h, :], ACT.Exp,
                                               bias=nmax0[g][:, p.par, h:h + 1], accum_out=den0[g][:, p.par, h:h + 1])
                ins.then_inc(sem(f"ex{g}"), 1)

            def copy_weights0(g, p):
                if not live(p):
                    return
                wait(act, f"ot{g}", p, back=1)
                wait(act, f"pt{g}", p)
                nc.scalar.activation(attnT0[g][:, :, :].rearrange("p h n -> p (h n)"), ps[:, bank_of[f"pt{g}"], :],
                                     ACT.Copy).then_inc(sem(f"pc{g}"), 1)

            def elu_exp0(g, p):
                if not live(p):
                    return
                wait(act, f"hl{g}", p, back=2)
                wait(act, f"ot{g}", p)
                nc.scalar.activation(hid[g][:, p.par, :], ps[:, bank_of[f"ot{g}"], :], ACT.Exp, bias=minus1[:, 0:1])\
                    .then_inc(sem(f"el{g}"), 1)

            def scaled(X, p):
                if not live(p):
                    return
                wait(act, "tk" if X == "D" else f"pt{X}", p, back=2)
                wait(act, f"z{X}", p)
                for g in range(G):
                    ins = nc.scalar.activation(graph_cols(prob[X], p.par, g), ps[:, bank_of[f"z{X}"], g * P:(g + 1) * P],
                                               ACT.Relu, scale=rise(SLOPE[X]), bias=val[X][:, p.par, g, ROW[X]:ROW[X] + 1])
                ins.then_inc(sem(f"az{X}"), 1)

            def exponentials(X, p):
                if not live(p):
                    return
                wait(act, f"ng{X}", p)
                for g in range(G):
                    src = ps[:, bank_of["sC"], g * P:(g + 1) * P] if X == "C" else graph_cols(prob[X], p.par, g)
                    ins = nc.scalar.activation(graph_cols(prob[X], p.par, g), src, ACT.Exp,
                                               bias=nmax[X][:, p.par, g:g + 1], accum_out=den[X][:, p.par, g:g + 1])
                ins.then_inc(sem(f"ex{X}"), 1)

            def copy_weights(X, p):
                if not live(p):
                    return
                wait(act, f"o{X}", p, back=1)
                wait(act, f"pt{X}", p)
                nc.scalar.activation(probT[X][:, :], ps[:, bank_of[f"pt{X}"], 0:G * NODES], ACT.Copy)\
                    .then_inc(sem(f"pc{X}"), 1)

            def copy_values(X, g, p):
                if not live(p):
                    return
                wait(act, f"w{X}{g}", p)
                nc.scalar.activation(val[X][:, p.par, g, :], ps[:, bank_of[f"w{X}{g}"], 0:DIM + 2], ACT.Copy)\
                    .then_inc(sem(f"wc{X}{g}"), 1)

            def copy_queries(p):
                if not live(p):
                    return
                wait(act, "sC", p, back=1)
                wait(act, "gt", p)
                for c in range(KC):
                    ins = nc.scalar.activation(qT[:, c, :], ps[:, bank_of["gt"], c * G * P:(c + 1) * G * P],
                                               ACT.Identity, bias=c_s[:, c:c + 1])
                ins.then_inc(sem("gc"), 1)

            def elu_exp(X, p):
                if not live(p):
                    return
                wait(act, f"fin{X}", p, back=2)
                wait(act, f"rd{X}", p)
                wait(act, f"o{X}", p)
                for g in range(G):
                    nc.scalar.activation(graph_cols(elu[X], p.par, g, DIM), ps[:, bank_of[f"o{X}"], g * DIM:(g + 1) * DIM],
                                               ACT.Exp, scale=rden[X][:, p.par, g:g + 1])

            def elu_relu(X, p):
                if not live(p):
                    return
                wait(act, f"t{X}", p, back=1)
                for g in range(G):
                    ins = nc.scalar.activation(pos[X][:, g * DIM:(g + 1) * DIM], ps[:, bank_of[f"o{X}"], g * DIM:(g + 1) * DIM],
                                               ACT.Relu, scale=rden[X][:, p.par, g:g + 1])
                ins.then_inc(sem(f"r{X}"), 1)

            def load(dst, src, into="weights_in", **how):
                act.dma_start(dst, src, **how).then_inc(sem(into), 16)

            load(w1_in, w1.rearrange("(c k) n -> k c n", k=P), "w1_in")
            load(rows1[:, 0, :], on_all(src1.rearrange("h f -> (h f)"), HID), "w1_in")
            load(rows1[:, 1, :], on_all(dst1.rearrange("h f -> (h f)"), HID), "w1_in")
            load(b1_s[:, :], on_all(b1, HID), "w1_in")

            load(w2_in[:, :, 0:DIM], w2.rearrange("(h f) o -> f h o", f=P))
            load(rows2[:, 0, :], on_all(src2.rearrange("h f -> (h f)"), DIM))
            load(rows2[:, 1, :], on_all(dst2.rearrange("h f -> (h f)"), DIM))
            load(b2_s[:, 0:DIM], on_all(b2, DIM))
            load(wl_in, wl.rearrange("(c k) i -> k c i", k=P))
            load(al_in, al.rearrange("(c k) j -> k c j", k=P))
            load(bl_col[:, :], bl.rearrange("(c k) -> k c", k=P), allow_slow_non_contiguous=True)
            load(bv_s[:, 0:DIM], on_all(bl, DIM))
            load(w3_in[:, :, 0:DIM], w3.rearrange("(c k) o -> k c o", k=P))
            load(rows34[:, 0, :], on_all(a3[0:DIM].rearrange("n a -> (n a)"), DIM))
            load(rows34[:, 1, :], on_all(a3[DIM:2 * DIM].rearrange("n a -> (n a)"), DIM))
            load(w4_in[:, :, 0:DIM], w4.rearrange("(c k) o -> k c o", k=P))
            load(rows34[:, 2, :], on_all(a4src.rearrange("n a -> (n a)"), DIM))
            load(rows34[:, 3, :], on_all(a4dst.rearrange("n a -> (n a)"), DIM))

            def round_high(dst, src):
                return nc.scalar.activation(dst, src, ACT.Copy)

            act.wait_ge(sem("w1_in"), 16 * W1_LOADS)
            round_high(w1_s[:, HIGH, :, :], w1_in).then_inc(sem("w1_high"), 1)
            act.wait_ge(sem("coef_made"), 1)
            round_high(coef_s[:, HIGH, :, :], coef_in).then_inc(sem("w1_high"), 1)

            def later_weights():
                act.wait_ge(sem("columns_made"), 1)
                for w, w_in in ((w2_s, w2_in), (w3_s, w3_in), (w4_s, w4_in)):
                    round_high(w[:, HIGH, :, :], w_in).then_inc(sem("weights_high"), 1)
                act.wait_ge(sem("c_copied"), 1)
                round_high(wv_s[:, HIGH, :, 0:DIM], ps[:, made_in["wl_turned"], :].rearrange("p (c n) -> p c n", c=KC))
                round_high(wv_s[:, HIGH, :, DIM:DIM + 1], c_s[:, KC:2 * KC].unsqueeze(2))
                round_high(m_s[:, HIGH, :, :], ps[:, made_in["m"], :].rearrange("p (c n) -> p c n", c=KC)).then_inc(sem("weights_high"), 1)
                act.wait_ge(sem("weights_ready"), 2)

            def turn(t):
                elu_relu("C", lagged(t, 3))
                copy_weights("E", lagged(t, 6))
                relu_copy(3, lagged(t, 5))
                scaled0(1, lagged(t, 1))
                exponentials("B", lagged(t, 2))
                copy_weights("D", lagged(t, 4))
                scaled0(0, lagged(t, 1))
                copy_weights("B", lagged(t, 2))
                exponentials0(1, lagged(t, 1))
                elu_exp("E", lagged(t, 6))
                copy_values("E", 1, lagged(t, 5))
                elu_relu("E", lagged(t, 6))
                copy_values("E", 0, lagged(t, 5))
                exponentials0(0, lagged(t, 1))
                relu_copy(2, lagged(t, 3))
                copy_weights0(1, lagged(t, 1))
                elu_exp("D", lagged(t, 4))
                relu_copy(1, lagged(t, 2))
                elu_relu("D", lagged(t, 4))
                copy_weights0(0, lagged(t, 1))
                scaled("E", lagged(t, 5))
                elu_exp0(1, lagged(t, 1))
                copy_values("D", 1, lagged(t, 3))
                copy_values("D", 0, lagged(t, 3))
                elu_exp0(0, lagged(t, 1))
                copy_queries(lagged(t, 2))
                exponentials("E", lagged(t, 5))
                relu_copy(0, lagged(t, 0))
                scaled("D", lagged(t, 3))
                exponentials("C", lagged(t, 2))
                split_high(lagged(t, 0))
                copy_weights("C", lagged(t, 2))
                split_middle(lagged(t, 0))
                exponentials("D", lagged(t, 3))
                elu_exp("C", lagged(t, 2))
                scaled("B", lagged(t, 1))

            over_turns(act, turn, later_weights)

        @block.vector
        def _(dve):
            made = sem("dve_made")
            steps = [0]

            def chain(ins):
                steps[0] += 1
                ins.then_inc(made, 1)
                dve.wait_ge(made, steps[0])

            def tt(o, a, b, op):
                return nc.vector.tensor_tensor(o, a, b, op)

            def low(w, w_high, w_in):
                return nc.vector.tensor_tensor(w, w_in, w_high.bitcast(F32), ALU.subtract)

            def later_weights():
                dve.wait_ge(sem("pe_made"), T1_SUM)
                nc.vector.tensor_copy(t1_s, ps[:, made_in["t1"], :].rearrange("p (c n) -> p c n", c=KC)).then_inc(sem("t1_ready"), 1)
                dve.wait_ge(sem("pe_made"), AB_SUM)
                nc.vector.tensor_copy(ab_s[:, :], ps[:, made_in["ab"], 0:KC]).then_inc(sem("t1_ready"), 1)
                products = 0
                for w_in, prods, factors in ((w2_in, prod2, (1.0, rise(SLOPE_L0))), (w3_in, prod3, (rise(SLOPE_L2), 1.0)),
                                             (w4_in, prod4, (rise(SLOPE_L3), 1.0))):
                    for j in range(2):
                        products += 1
                        dve.wait_ge(sem("multiplied"), products)
                        ins = nc.vector.tensor_reduce(w_in[:, :, DIM + j], prods[j], AX.X, ALU.add)
                        if factors[j] != 1:
                            chain(ins)
                            ins = nc.vector.tensor_scalar(w_in[:, :, DIM + j], w_in[:, :, DIM + j], factors[j], None, ALU.mult)
                nc.vector.memset(wv_s[:, :, :, DIM + 1:DIM + 2].bitcast(F32), 0.0).then_inc(sem("columns_made"), 1)
                dve.wait_ge(sem("pe_made"), C_SUM)
                nc.vector.tensor_copy(bv_s[:, DIM:DIM + 1], ps[:, made_in["c"], 2 * KC:2 * KC + 1])
                nc.vector.tensor_copy(c_s[:, :], ps[:, made_in["c"], 0:2 * KC]).then_inc(sem("c_copied"), 1)
                dve.wait_ge(sem("pe_made"), W2_SUM)
                nc.vector.scalar_tensor_tensor(out=b2_s[:, 0:DIM], in0=b2_s[:, 0:DIM], scalar=-3.0, in1=ps[:, made_in["w2_sum"], 0:DIM],
                                               op0=ALU.add, op1=ALU.subtract)
                nc.vector.tensor_scalar(b2_s[:, DIM:DIM + 2], ps[:, made_in["w2_sum"], DIM:DIM + 2], -1.0, None, ALU.mult)
                dve.wait_ge(sem("weights_high"), 4)
                low(wv_s[:, LOW, :, 0:DIM], wv_s[:, HIGH, :, 0:DIM], ps[:, made_in["wl_turned"], :].rearrange("p (c n) -> p c n", c=KC))
                low(wv_s[:, LOW, :, DIM:DIM + 1], wv_s[:, HIGH, :, DIM:DIM + 1], c_s[:, KC:2 * KC].unsqueeze(2))
                low(m_s[:, LOW, :, :], m_s[:, HIGH, :, :], ps[:, made_in["m"], :].rearrange("p (c n) -> p c n", c=KC))\
                    .then_inc(sem("weights_ready"), 1)
                dve.wait_ge(sem("weights_ready"), 2)

            def gone_ahead(k, p):
                return k == 0 and isinstance(p.n, int) and p.n == 0

            def wait_apart(p):
                if not isinstance(p.n, int):
                    dve.wait_ge(sem("w1_ready"), 1)

            def statistics(k, p, ahead=False):
                if not live(p) or (gone_ahead(k, p) and not ahead):
                    return
                if k == 0:
                    dve.wait_ge(sem(f"x_in{p.par}"), dma_count(p))
                else:
                    wait(dve, {1: "rsB", 2: "finC", 3: "finD"}[k], p)
                for g in range(G):
                    ins = nc.vector.bn_stats(stats[k][:, p.par, g, :], res[k][:, p.par, g, :])
                ins.then_inc(sem(f"stat{k}"), 1)

            def mean_and_variance(k, p, ahead=False):
                if not live(p) or (gone_ahead(k, p) and not ahead):
                    return
                have(dve, p.n + 1)
                wait_apart(p)
                wait(dve, f"stat{k}", p)
                for g in range(G):
                    ins = nc.vector.bn_aggr(mv[k][:, p.par, g, :], stats[k][:, p.par, g, :])
                ins.then_inc(sem(f"aggr{k}"), 1)

            def negative_mean(k, p, ahead=False):
                if not live(p) or (gone_ahead(k, p) and not ahead):
                    return
                wait(dve, f"aggr{k}", p)
                nc.vector.tensor_scalar(nmean[k][:, p.par, :], mv[k][:, p.par, :, 0], -1.0, None, ALU.mult)
                nc.vector.tensor_scalar(vare[k][:, p.par, :], mv[k][:, p.par, :, 1], EPS, None, ALU.add)\
                    .then_inc(sem(f"aggr{k}"), 1)

            def make_masks(p):
                if not live(p):
                    return
                dve.wait_ge(sem(f"adj_in{p.par}"), dma_count(p))
                nc.vector.scalar_tensor_tensor(out=mask0[:, p.par, :, :], in0=adj_s[:, p.par, :, :], scalar=0.0,
                                               in1=offdiag[:, :].unsqueeze(1).to_broadcast([P, G, P]),
                                               op0=ALU.is_le, op1=ALU.mult)
                mine = masks[:, G * p.n:G * p.n + G, :] if isinstance(p.n, int) else masks[:, bass.ds(p.n * G, G), :]
                nc.vector.tensor_scalar(mine, adj_s[:, p.par, :, :], 0.0, NEG, ALU.is_equal, ALU.mult)\
                    .then_inc(sem("mk"), 1)

            def split_rest(p):
                if not live(p):
                    return
                wait(dve, "sp0", p)
                nc.vector.tensor_tensor(rest[MID:P, p.par, :], ps[MID:P, bank_of["as"], 0:G * NODES], parts[MID:P, p.par, :],
                                        ALU.subtract).then_inc(sem("sp1"), 1)

            def split_low(p):
                if not live(p):
                    return
                wait(dve, "sp1b", p)
                nc.vector.tensor_tensor(parts[LO:P, p.par, :], rest[LO:P, p.par, :], parts[LO:P, p.par, :], ALU.subtract)\
                    .then_inc(sem("sp2"), 1)

            def bias_values0(g, p):
                if not live(p):
                    return
                wait(dve, f"xl{g}", p)
                tt(val0[g][:, p.par, :], ps[:, bank_of[f"xl{g}"], :], b1_s[:, :], ALU.add).then_inc(sem(f"xb{g}"), 1)

            def leaky_and_maximum(out_, z, slope, largest):
                return nc.vector.tensor_tensor_reduce(out_, z, out_, slope, LOWEST, ALU.add, ALU.max, largest)

            def maximum0(g, p):
                if not live(p):
                    return
                have(dve, p.n + 1)
                wait_apart(p)
                wait(dve, f"az{g}", p)
                for h in range(HEADS):
                    ins = leaky_and_maximum(attn0[g][:, p.par, h, :], ps[:, bank_of[f"z{g}"], h * P:(h + 1) * P],
                                            SLOPE_L0, den0[g][:, p.par, h:h + 1])
                ins.then_inc(sem(f"mx{g}"), 1)

            def negative_maximum0(g, p):
                if not live(p):
                    return
                wait(dve, f"mx{g}", p)
                nc.vector.tensor_scalar(nmax0[g][:, p.par, :], den0[g][:, p.par, :], -1.0, None, ALU.mult).then_inc(sem(f"mx{g}"), 1)

            def reciprocal0(g, p):
                if not live(p):
                    return
                wait(dve, f"ex{g}", p)
                nc.vector.reciprocal(rden0[g][:, p.par, :], den0[g][:, p.par, :]).then_inc(sem(f"rd{g}"), 1)

            def elu0(g, p):
                if not live(p):
                    return
                wait(dve, f"el{g}", p)
                nc.vector.scalar_tensor_tensor(out=hid[g][:, p.par, :], in0=hid[g][:, p.par, :], scalar=1.0,
                                               in1=ps[:, bank_of[f"ot{g}"], :], op0=ALU.min, op1=ALU.max)\
                    .then_inc(sem(f"eu{g}"), 1)

            def low_h(k, p):
                if not live(p):
                    return
                wait(dve, f"rl{k}", p)
                nc.vector.scalar_tensor_tensor(out=flat2(hT[k][:, LOW, :, :]), in0=ps[:, bank_of[f"tr{k}"], :], scalar=0.0,
                                               in1=flat2(hT[k][:, HIGH, :, :]).bitcast(F32), op0=ALU.max, op1=ALU.subtract)\
                    .then_inc(sem(f"lo{k}"), 1)

            def high_h1(p):
                if not live(p):
                    return
                wait(dve, "v1", p, back=1)
                wait(dve, "rl1", p)
                nc.vector.tensor_copy(flat2(hT[1][:, HIGH, :, :]), flat2(hT1[:, p.par, :, :])).then_inc(sem("hi1"), 1)

            def high_hid(g, p):
                if not live(p):
                    return
                wait(dve, f"xm{g}", p, back=1)
                wait(dve, f"eu{g}", p)
                nc.vector.tensor_copy(hid_r[g][:, HIGH, :], hid[g][:, p.par, :]).then_inc(sem(f"hh{g}"), 1)

            def bias_values(X, g, p):
                if not live(p):
                    return
                src, dst_sem, bias, n = {"B": (f"xm{g}", f"xn{g}", b2_s, DIM + 2), "C": (f"v{g}", f"vb{g}", bv_s, DIM + 1)}[X]
                wait(dve, src, p)
                tt(val[X][:, p.par, g, 0:n], ps[:, bank_of[src], 0:n], bias[:, :], ALU.add).then_inc(sem(dst_sem), 1)

            def maximum(X, p):
                if not live(p):
                    return
                if X == "C":
                    wait(dve, "sC", p)
                    nc.vector.tensor_reduce(mx[X][:, p.par, :], ps[:, bank_of["sC"], 0:G * NODES].rearrange("p (g n) -> p g n", g=G),
                                            AX.X, ALU.max).then_inc(sem("mxC"), 1)
                else:
                    have(dve, p.n + 1)
                    wait_apart(p)
                    wait(dve, f"az{X}", p)
                    for g in range(G):
                        ins = leaky_and_maximum(graph_cols(prob[X], p.par, g), ps[:, bank_of[f"z{X}"], g * P:(g + 1) * P],
                                                SLOPE[X], mx[X][:, p.par, g:g + 1])
                    ins.then_inc(sem(f"mx{X}"), 1)

            def negative_maximum(X, p):
                if not live(p):
                    return
                wait(dve, f"mx{X}", p)
                nc.vector.tensor_scalar(nmax[X][:, p.par, :], mx[X][:, p.par, :], -1.0, None, ALU.mult).then_inc(sem(f"mx{X}"), 1)

            def reciprocal(X, p):
                if not live(p):
                    return
                wait(dve, f"ex{X}", p)
                nc.vector.reciprocal(rden[X][:, p.par, :], den[X][:, p.par, :]).then_inc(sem(f"rd{X}"), 1)

            def residual_b(p):
                if not live(p):
                    return
                wait(dve, "finC", p, back=2)
                wait(dve, "rdB", p)
                wait(dve, "oB", p)
                for g in range(G):
                    ins = nc.vector.scalar_tensor_tensor(out=res[1][:, p.par, g, :], in0=ps[:, bank_of["oB"], g * DIM:(g + 1) * DIM],
                                                         scalar=rden["B"][:, p.par, g:g + 1], in1=res[0][:, p.par, g, :],
                                                         op0=ALU.mult, op1=ALU.add)
                ins.then_inc(sem("rsB"), 1)

            def keep_top(p):
                if not live(p):
                    return
                exps = [graph_cols(prob["D"], p.par, g) for g in range(G)]
                largest = [[top[g][:, p.par, r, :] for g in range(G)] for r in range(TOPK_ROUNDS)]
                rest_of = [left[g][:, p.par, :] for g in range(G)]
                have(dve, p.n + 1, p.n * 3 + 1, p.n * 3 + 2, p.n * 3 + 3)

                def done(g, count):
                    wait_apart(p)
                    dve.wait_ge(sem(f"top_{g}"), p.n * 3 + count)

                wait_apart(p)
                wait(dve, "exD", p)
                for g in range(G):
                    nc.vector.max(largest[0][g], exps[g]).then_inc(sem(f"top_{g}"), 1)
                for g in range(G):
                    done(g, 1)
                    nc.vector.match_replace(rest_of[g], largest[0][g], exps[g], -1.0).then_inc(sem(f"top_{g}"), 1)
                for g in range(G):
                    done(g, 2)
                    nc.vector.max(largest[1][g], rest_of[g]).then_inc(sem(f"top_{g}"), 1)
                for g in range(G):
                    dve.wait_ge(sem(f"top_{g}"), p.n * 3 + 3)
                    ins = nc.vector.scalar_tensor_tensor(out=graph_cols(kept, p.par, g), in0=exps[g], scalar=largest[1][g][:, 7:8],
                                                         in1=exps[g], op0=ALU.is_ge, op1=ALU.mult)
                ins.then_inc(sem("tk"), 1)

            def elu_sum(X, p):
                if not live(p):
                    return
                wait(dve, f"r{X}", p)
                nc.vector.scalar_tensor_tensor(out=elu[X][:, p.par, :], in0=elu[X][:, p.par, :], scalar=1.0,
                                               in1=pos[X][:, :], op0=ALU.min, op1=ALU.add).then_inc(sem(f"t{X}"), 1)

            chain(nc.vector.memset(coef_in, 0.0))
            first = Pair(0, 0)
            for step in (statistics, mean_and_variance, negative_mean):
                step(0, first, ahead=True)
            dve.wait_ge(sem("w1_in"), 16 * W1_LOADS)

            for j in range(2):
                for c in range(KC):
                    chain(tt(prod1, w1_in[:, c, :], rows1[:, j, :], ALU.mult))
                    chain(nc.vector.tensor_reduce(coef_in[:, c, HI + j * HEADS:HI + (j + 1) * HEADS],
                                                  prod1.rearrange("p (h f) -> p h f", f=HF), AX.X, ALU.add))
            for start in (MID, LO):
                ins = nc.vector.tensor_copy(coef_in[:, :, start:start + 2 * HEADS], coef_in[:, :, HI:HI + 2 * HEADS])
            ins.then_inc(sem("coef_made"), 1)
            nc.vector.tensor_scalar(b1_s[:, :], b1_s[:, :], 1.0, None, ALU.add)
            dve.wait_ge(sem("w1_high"), 2)
            dve.wait_ge(sem("coef_made"), 1)
            low(w1_s[:, LOW, :, :], w1_s[:, HIGH, :, :], w1_in)
            low(coef_s[:, LOW, :, :], coef_s[:, HIGH, :, :], coef_in).then_inc(sem("w1_ready"), 1)
            dve.wait_ge(sem("w1_ready"), 1)
            dve.wait_ge(sem("constants"), 1)

            def turn(t):
                keep_top(lagged(t, 4))
                maximum("B", lagged(t, 2))
                elu_sum("C", lagged(t, 3))
                negative_maximum("B", lagged(t, 2))
                low_h(3, lagged(t, 5))
                maximum0(1, lagged(t, 1))
                statistics(2, lagged(t, 3))
                negative_maximum0(1, lagged(t, 1))
                mean_and_variance(2, lagged(t, 3))
                reciprocal("B", lagged(t, 2))
                reciprocal("E", lagged(t, 6))
                negative_mean(2, lagged(t, 3))
                maximum0(0, lagged(t, 1))
                residual_b(lagged(t, 2))
                reciprocal0(1, lagged(t, 1))
                statistics(1, lagged(t, 2))
                reciprocal("D", lagged(t, 4))
                mean_and_variance(1, lagged(t, 2))
                negative_maximum0(0, lagged(t, 1))
                negative_mean(1, lagged(t, 2))
                bias_values0(1, lagged(t, 1))
                bias_values0(0, lagged(t, 1))
                reciprocal0(0, lagged(t, 1))
                elu_sum("E", lagged(t, 6))
                low_h(2, lagged(t, 3))
                statistics(0, lagged(t, 0))
                high_h1(lagged(t, 2))
                elu_sum("D", lagged(t, 4))
                mean_and_variance(0, lagged(t, 0))
                maximum("E", lagged(t, 5))
                negative_maximum("E", lagged(t, 5))
                negative_mean(0, lagged(t, 0))
                elu0(1, lagged(t, 1))
                high_hid(1, lagged(t, 1))
                statistics(3, lagged(t, 4))
                elu0(0, lagged(t, 1))
                bias_values("C", 0, lagged(t, 2))
                bias_values("C", 1, lagged(t, 2))
                mean_and_variance(3, lagged(t, 4))
                high_hid(0, lagged(t, 1))
                maximum("C", lagged(t, 2))
                low_h(0, lagged(t, 0))
                make_masks(lagged(t, 0))
                bias_values("B", 1, lagged(t, 1))
                maximum("D", lagged(t, 3))
                negative_mean(3, lagged(t, 4))
                split_rest(lagged(t, 0))
                negative_maximum("D", lagged(t, 3))
                reciprocal("C", lagged(t, 2))
                bias_values("B", 0, lagged(t, 1))
                split_low(lagged(t, 0))

            over_turns(dve, turn, later_weights)


_INS = ['x', 'adj', 'L0_gnn_W1', 'L0_gnn_att_src1', 'L0_gnn_att_dst1', 'L0_gnn_b1', 'L0_gnn_W2', 'L0_gnn_att_src2',
        'L0_gnn_att_dst2', 'L0_gnn_b2', 'L1_gnn_W', 'L1_gnn_b', 'L1_gnn_attn', 'L2_gnn_W', 'L2_gnn_a', 'L3_gnn_w',
        'L3_gnn_a1', 'L3_gnn_a2']


def kernel(**inputs):
    import concourse.bacc as bacc
    from concourse.bass_utils import run_bass_kernel_spmd

    nc = bacc.Bacc("TRN2", target_bir_lowering=False, num_devices=1)
    arrays, args = {}, []
    for name in _INS:
        a = np.ascontiguousarray(inputs[name])
        arrays[f"in_{name}"] = a
        args.append(nc.dram_tensor(f"in_{name}", a.shape, mybir.dt.from_np(a.dtype), kind="ExternalInput").ap())
    out = nc.dram_tensor("out", (GRAPHS, NODES, DIM), F32, kind="ExternalOutput").ap()
    graph_layers(nc, *args, out)
    return run_bass_kernel_spmd(nc, [arrays], core_ids=[0]).results[0]["out"]
```
